# Optimizing a Trainium2 kernel written in Bass

```python
import numpy as np
import jax
import jax.numpy as jnp

def _softmax(x, axis=-1):
    return jax.nn.softmax(x, axis=axis)

def _gelu(x):
    return jax.nn.gelu(x, approximate=True)

def _silu(x):
    return jax.nn.silu(x)

def _sigmoid(x):
    return jax.nn.sigmoid(x)

def _layernorm(x, axis=-1, eps=1e-05):
    m = jnp.mean(x, axis=axis, keepdims=True)
    v = jnp.var(x, axis=axis, keepdims=True)
    return (x - m) / jnp.sqrt(v + eps)

def _scatter_add(tgt, idx, src, axis=0):
    return tgt.at[idx].add(src)

def _segment_sum(src, seg, n):
    return jax.ops.segment_sum(src, seg, n)
kernel_name = 'mk_gnn_resnorm_d2_gnn_r64_eb598a'

def setup_inputs(seed: int=0):
    np.random.seed(seed)
    _w = jnp.asarray

    def _rec_inputs():
        import jax
        import jax.numpy as jnp
        _gk = jax.random.key(seed)
        x = -0.0009044 + 1 * jax.random.normal(jax.random.fold_in(_gk, 1), (100000, 160), jnp.float32)
        src = jax.random.randint(jax.random.fold_in(_gk, 2), (25000,), 0, 100000, jnp.int32)
        dst = jnp.minimum((100000 * jax.random.uniform(jax.random.fold_in(_gk, 3), (25000,)) ** 2.0).astype(jnp.int32), 99999)
        _o = jnp.argsort(dst, stable=True)
        src = src[_o]
        dst = dst[_o]
        edge_attr_3 = 0.00047201 + 1.00023 * jax.random.normal(jax.random.fold_in(_gk, 12), (25000, 3), jnp.float32)
        edge_attr_4 = -0.000414295 + 0.999828 * jax.random.normal(jax.random.fold_in(_gk, 13), (25000, 4), jnp.float32)
        edge_attr_64 = 0.000279952 + 1.00013 * jax.random.normal(jax.random.fold_in(_gk, 14), (25000, 64), jnp.float32)
        edge_attr_8 = jax.random.uniform(jax.random.fold_in(_gk, 15), (25000, 8), jnp.float32, 0.0, 1)
        node_vec1 = jax.random.uniform(jax.random.fold_in(_gk, 17), (100000, 1), jnp.float32, 0.0, 1)
        return (x, src, dst, edge_attr_3, edge_attr_4, edge_attr_64, edge_attr_8, node_vec1)
    x, src, dst, edge_attr_3, edge_attr_4, edge_attr_64, edge_attr_8, node_vec1 = _rec_inputs()

    def _L0_gnn_setup():
        import jax, jax.numpy as jnp
        import numpy as np
        N_NODES = 10000
        N_EDGES = 5000
        MUL0, MUL1 = (64, 32)
        EDGE_DIM = 64
        W_NUMEL = 224
        DENOM = 32.0
        SQRT3 = 3.0 ** 0.5
        INV_SQRT3 = 1.0 / SQRT3
        INV_SQRT2 = 2.0 ** (-0.5)

        def _forward(node_feature, edge_attr, edge_feature, W_skip0, W_skip1, W_nl0, W_nl1, W_fc1, W_fc2, W_out_s, W_out_v, edge_index):
            N = node_feature.shape[0]
            E = edge_attr.shape[0]
            s = node_feature[:, :MUL0]
            v = node_feature[:, MUL0:].reshape(N, MUL1, 3)
            skip_s = s @ W_skip0
            skip_v = jnp.einsum('nmi,mk->nki', v, W_skip1)
            s = s @ W_nl0
            v = jnp.einsum('nmi,mk->nki', v, W_nl1)
            rhat = edge_attr / jnp.linalg.norm(edge_attr, axis=-1, keepdims=True)
            sh1 = SQRT3 * rhat
            w = jax.nn.relu(edge_feature @ W_fc1) @ W_fc2
            w0, w1, w2, w3, w4 = jnp.split(w, [64, 128, 160, 192], axis=-1)
            src, dst = (edge_index[0], edge_index[1])
            xs = s[dst]
            xv = v[dst]
            out0a = w0 * xs
            out0b = w3 * (jnp.einsum('emi,ei->em', xv, sh1) * INV_SQRT3)
            out1a = (w1 * xs)[:, :, None] * sh1[:, None, :]
            out1b = w2[:, :, None] * xv
            out1c = w4[:, :, None] * (jnp.cross(xv, sh1[:, None, :]) * INV_SQRT2)
            tp = jnp.concatenate([out0a, out0b, out1a.reshape(E, -1), out1b.reshape(E, -1), out1c.reshape(E, -1)], axis=-1)
            agg = jax.ops.segment_sum(tp, src, num_segments=N) / DENOM
            agg_s = agg[:, :96]
            agg_v = agg[:, 96:].reshape(N, 128, 3)
            out_s = agg_s @ W_out_s + skip_s
            out_v = jnp.einsum('nmi,mk->nki', agg_v, W_out_v) + skip_v
            fs = jax.nn.silu(out_s[:, :MUL0])
            gate = jax.nn.sigmoid(out_s[:, MUL0:MUL0 + 32])
            gv = gate[:, :, None] * out_v
            return jnp.concatenate([fs, gv.reshape(N, -1)], axis=-1)
        key = jax.random.key(seed)
        ks = jax.random.split(key, 12)

        def lin(k, fi, fo):
            return jax.random.normal(k, (fi, fo), jnp.float32) / np.float32(np.sqrt(fi))
        return {'node_feature': jax.random.normal(ks[0], (N_NODES, MUL0 + 3 * MUL1), jnp.float32), 'edge_attr': jax.random.normal(ks[1], (N_EDGES, 3), jnp.float32), 'edge_feature': jax.random.normal(ks[2], (N_EDGES, EDGE_DIM), jnp.float32), 'W_skip0': lin(ks[3], MUL0, 96), 'W_skip1': lin(ks[4], MUL1, 32), 'W_nl0': lin(ks[5], MUL0, MUL0), 'W_nl1': lin(ks[6], MUL1, MUL1), 'W_fc1': lin(ks[7], EDGE_DIM, 64), 'W_fc2': lin(ks[8], 64, W_NUMEL), 'W_out_s': lin(ks[9], 96, 96), 'W_out_v': lin(ks[10], 128, 32), 'edge_index': jax.random.randint(ks[11], (2, N_EDGES), 0, N_NODES)}
    _L0_gnn_all = _L0_gnn_setup()
    _L0_gnn_in = {k: v for k, v in _L0_gnn_all.items() if k in ('W_skip0', 'W_skip1', 'W_nl0', 'W_nl1', 'W_fc1', 'W_fc2', 'W_out_s', 'W_out_v')}
    del _L0_gnn_all

    def _L1_gnn_setup():
        import jax, jax.numpy as jnp
        import numpy as np
        N = 625
        E = 6250
        MUL0, MUL1 = (64, 32)
        RAD, HID = (8, 64)
        WNUM = 192
        NUM_NEIGHBORS = 10.0
        INV3 = 1.0 / np.sqrt(3.0)

        def _lin(s, v, Ws, Wv, attr):
            out_s = s @ Ws * attr * (1.0 / np.sqrt(Ws.shape[0]))
            out_v = jnp.einsum('nud,uv->nvd', v, Wv) * attr[..., None] * (1.0 / np.sqrt(Wv.shape[0]))
            return (out_s, out_v)
        key = jax.random.key(seed)
        ks = jax.random.split(key, 16)
        return {'node_input': jax.random.normal(ks[0], (N, MUL0 + 3 * MUL1), jnp.float32), 'node_attr': jnp.ones((N, 1), jnp.float32), 'edge_attr': jax.random.normal(ks[1], (E, 4), jnp.float32), 'edge_scalars': jax.random.uniform(ks[2], (E, RAD), jnp.float32), 'W_sc_s': jax.random.normal(ks[3], (MUL0, MUL0), jnp.float32), 'W_sc_v': jax.random.normal(ks[4], (MUL1, MUL1), jnp.float32), 'W1_s': jax.random.normal(ks[5], (MUL0, MUL0), jnp.float32), 'W1_v': jax.random.normal(ks[6], (MUL1, MUL1), jnp.float32), 'W2_s': jax.random.normal(ks[7], (MUL0 + MUL1, MUL0), jnp.float32), 'W2_v': jax.random.normal(ks[8], (MUL0 + MUL1, MUL1), jnp.float32), 'W3': jax.random.normal(ks[9], (MUL0 + MUL1, 1), jnp.float32), 'fcW1': jax.random.normal(ks[10], (RAD, HID), jnp.float32), 'fcW2': jax.random.normal(ks[11], (HID, WNUM), jnp.float32), 'edge_src': jax.random.randint(ks[12], (E,), 0, N, jnp.int32), 'edge_dst': jax.random.randint(ks[13], (E,), 0, N, jnp.int32)}
    _L1_gnn_all = _L1_gnn_setup()
    _L1_gnn_in = {k: v for k, v in _L1_gnn_all.items() if k in ('W_sc_s', 'W_sc_v', 'W1_s', 'W1_v', 'W2_s', 'W2_v', 'W3', 'fcW1', 'fcW2')}
    del _L1_gnn_all
    return {'x': x, 'src': src, 'dst': dst, 'edge_attr_3': edge_attr_3, 'edge_attr_4': edge_attr_4, 'edge_attr_64': edge_attr_64, 'edge_attr_8': edge_attr_8, 'node_vec1': node_vec1, 'L0_gnn_W_skip0': _L0_gnn_in['W_skip0'], 'L0_gnn_W_skip1': _L0_gnn_in['W_skip1'], 'L0_gnn_W_nl0': _L0_gnn_in['W_nl0'], 'L0_gnn_W_nl1': _L0_gnn_in['W_nl1'], 'L0_gnn_W_fc1': _L0_gnn_in['W_fc1'], 'L0_gnn_W_fc2': _L0_gnn_in['W_fc2'], 'L0_gnn_W_out_s': _L0_gnn_in['W_out_s'], 'L0_gnn_W_out_v': _L0_gnn_in['W_out_v'], 'L1_gnn_W_sc_s': _L1_gnn_in['W_sc_s'], 'L1_gnn_W_sc_v': _L1_gnn_in['W_sc_v'], 'L1_gnn_W1_s': _L1_gnn_in['W1_s'], 'L1_gnn_W1_v': _L1_gnn_in['W1_v'], 'L1_gnn_W2_s': _L1_gnn_in['W2_s'], 'L1_gnn_W2_v': _L1_gnn_in['W2_v'], 'L1_gnn_W3': _L1_gnn_in['W3'], 'L1_gnn_fcW1': _L1_gnn_in['fcW1'], 'L1_gnn_fcW2': _L1_gnn_in['fcW2']}

def reference(x, src, dst, edge_attr_3, edge_attr_4, edge_attr_64, edge_attr_8, node_vec1, L0_gnn_W_skip0, L0_gnn_W_skip1, L0_gnn_W_nl0, L0_gnn_W_nl1, L0_gnn_W_fc1, L0_gnn_W_fc2, L0_gnn_W_out_s, L0_gnn_W_out_v, L1_gnn_W_sc_s, L1_gnn_W_sc_v, L1_gnn_W1_s, L1_gnn_W1_v, L1_gnn_W2_s, L1_gnn_W2_v, L1_gnn_W3, L1_gnn_fcW1, L1_gnn_fcW2):
    import jax
    import jax.numpy as jnp

    def _L0_gnn_ref(node_feature, edge_attr, edge_feature, W_skip0, W_skip1, W_nl0, W_nl1, W_fc1, W_fc2, W_out_s, W_out_v, edge_index):
        import jax, jax.numpy as jnp
        import numpy as np
        N_NODES = 10000
        N_EDGES = 5000
        MUL0, MUL1 = (64, 32)
        EDGE_DIM = 64
        W_NUMEL = 224
        DENOM = 32.0
        SQRT3 = 3.0 ** 0.5
        INV_SQRT3 = 1.0 / SQRT3
        INV_SQRT2 = 2.0 ** (-0.5)

        def _forward(node_feature, edge_attr, edge_feature, W_skip0, W_skip1, W_nl0, W_nl1, W_fc1, W_fc2, W_out_s, W_out_v, edge_index):
            N = node_feature.shape[0]
            E = edge_attr.shape[0]
            s = node_feature[:, :MUL0]
            v = node_feature[:, MUL0:].reshape(N, MUL1, 3)
            skip_s = s @ W_skip0
            skip_v = jnp.einsum('nmi,mk->nki', v, W_skip1)
            s = s @ W_nl0
            v = jnp.einsum('nmi,mk->nki', v, W_nl1)
            rhat = edge_attr / jnp.linalg.norm(edge_attr, axis=-1, keepdims=True)
            sh1 = SQRT3 * rhat
            w = jax.nn.relu(edge_feature @ W_fc1) @ W_fc2
            w0, w1, w2, w3, w4 = jnp.split(w, [64, 128, 160, 192], axis=-1)
            src, dst = (edge_index[0], edge_index[1])
            xs = s[dst]
            xv = v[dst]
            out0a = w0 * xs
            out0b = w3 * (jnp.einsum('emi,ei->em', xv, sh1) * INV_SQRT3)
            out1a = (w1 * xs)[:, :, None] * sh1[:, None, :]
            out1b = w2[:, :, None] * xv
            out1c = w4[:, :, None] * (jnp.cross(xv, sh1[:, None, :]) * INV_SQRT2)
            tp = jnp.concatenate([out0a, out0b, out1a.reshape(E, -1), out1b.reshape(E, -1), out1c.reshape(E, -1)], axis=-1)
            agg = jax.ops.segment_sum(tp, src, num_segments=N) / DENOM
            agg_s = agg[:, :96]
            agg_v = agg[:, 96:].reshape(N, 128, 3)
            out_s = agg_s @ W_out_s + skip_s
            out_v = jnp.einsum('nmi,mk->nki', agg_v, W_out_v) + skip_v
            fs = jax.nn.silu(out_s[:, :MUL0])
            gate = jax.nn.sigmoid(out_s[:, MUL0:MUL0 + 32])
            gv = gate[:, :, None] * out_v
            return jnp.concatenate([fs, gv.reshape(N, -1)], axis=-1)
        return _forward(node_feature, edge_attr, edge_feature, W_skip0, W_skip1, W_nl0, W_nl1, W_fc1, W_fc2, W_out_s, W_out_v, edge_index)

    def _L1_gnn_ref(node_input, node_attr, edge_attr, edge_scalars, W_sc_s, W_sc_v, W1_s, W1_v, W2_s, W2_v, W3, fcW1, fcW2, edge_src, edge_dst):
        import jax, jax.numpy as jnp
        import numpy as np
        N = 625
        E = 6250
        MUL0, MUL1 = (64, 32)
        RAD, HID = (8, 64)
        WNUM = 192
        NUM_NEIGHBORS = 10.0
        INV3 = 1.0 / np.sqrt(3.0)

        def _lin(s, v, Ws, Wv, attr):
            out_s = s @ Ws * attr * (1.0 / np.sqrt(Ws.shape[0]))
            out_v = jnp.einsum('nud,uv->nvd', v, Wv) * attr[..., None] * (1.0 / np.sqrt(Wv.shape[0]))
            return (out_s, out_v)
        n = node_input.shape[0]
        s_in = node_input[:, :MUL0]
        v_in = node_input[:, MUL0:].reshape(n, MUL1, 3)
        sc_s, sc_v = _lin(s_in, v_in, W_sc_s, W_sc_v, node_attr)
        f_s, f_v = _lin(s_in, v_in, W1_s, W1_v, node_attr)
        h = jax.nn.silu(edge_scalars @ fcW1 * (1.0 / np.sqrt(RAD)))
        w = h @ fcW2 * (1.0 / np.sqrt(HID))
        wA, wB, wC, wD = (w[:, :64], w[:, 64:128], w[:, 128:160], w[:, 160:192])
        xs = f_s[edge_src]
        xv = f_v[edge_src]
        y0 = edge_attr[:, :1]
        y1 = edge_attr[:, 1:4]
        outA = wA * xs * y0
        outD = wD * jnp.einsum('eud,ed->eu', xv, y1) * INV3
        outB = wB[:, :, None] * xs[:, :, None] * y1[:, None, :]
        outC = wC[:, :, None] * xv * y0[:, :, None]
        edge_feat = jnp.concatenate([outA, outD, outB.reshape(-1, MUL0 * 3), outC.reshape(-1, MUL1 * 3)], axis=1)
        agg = jax.ops.segment_sum(edge_feat, edge_dst, num_segments=n)
        agg = agg * (1.0 / np.sqrt(NUM_NEIGHBORS))
        ms = agg[:, :MUL0 + MUL1]
        mv = agg[:, MUL0 + MUL1:].reshape(n, MUL0 + MUL1, 3)
        c_s, c_v = _lin(ms, mv, W2_s, W2_v, node_attr)
        conv = jnp.concatenate([c_s, c_v.reshape(n, -1)], axis=1)
        sc = jnp.concatenate([sc_s, sc_v.reshape(n, -1)], axis=1)
        angle = 0.1 * (ms @ W3) * node_attr * (1.0 / np.sqrt(MUL0 + MUL1))
        cos, sin = (jnp.cos(angle), jnp.sin(angle))
        return cos * sc + sin * conv
    edge_index = jnp.stack([src, dst])
    x = _layernorm(x + _L0_gnn_ref(x, edge_attr_3, edge_attr_64, L0_gnn_W_skip0, L0_gnn_W_skip1, L0_gnn_W_nl0, L0_gnn_W_nl1, L0_gnn_W_fc1, L0_gnn_W_fc2, L0_gnn_W_out_s, L0_gnn_W_out_v, edge_index), axis=-1)
    x = _layernorm(x + _L1_gnn_ref(x, node_vec1, edge_attr_4, edge_attr_8, L1_gnn_W_sc_s, L1_gnn_W_sc_v, L1_gnn_W1_s, L1_gnn_W1_v, L1_gnn_W2_s, L1_gnn_W2_v, L1_gnn_W3, L1_gnn_fcW1, L1_gnn_fcW2, src, dst), axis=-1)
    return x

_drawn_inputs = setup_inputs


def setup_inputs(seed=0):
    import zlib

    import numpy as np

    out = dict(_drawn_inputs(seed))
    spreads = {}
    factors = {'edge_attr_3': 8.0,
     'edge_attr_4': 8.0,
     'edge_attr_64': 8.0,
     'edge_attr_8': 8.0,
     'L0_gnn_W_nl0': 8.0,
     'L0_gnn_W_nl1': 8.0,
     'L0_gnn_W_fc1': 8.0,
     'L0_gnn_W_fc2': 8.0,
     'L0_gnn_W_out_s': 8.0,
     'L0_gnn_W_out_v': 8.0,
     'L1_gnn_W1_s': 8.0,
     'L1_gnn_W1_v': 8.0,
     'L1_gnn_W2_s': 8.0,
     'L1_gnn_W2_v': 8.0,
     'L1_gnn_W3': 8.0,
     'L1_gnn_fcW1': 8.0,
     'L1_gnn_fcW2': 8.0}
    for name, (base, spread) in spreads.items():
        noise = np.random.default_rng([zlib.crc32(name.encode()), seed]).standard_normal(out[name].shape)
        drawn = base * np.exp(spread * noise) if base else spread * noise
        out[name] = jnp.asarray(drawn.astype(out[name].dtype))
    for name, factor in factors.items():
        out[name] = (out[name] * factor).astype(out[name].dtype)
    return out
```

```python
import concourse.bass as bass
from concourse import mybir
from contextlib import ExitStack

P = 128
N_NODES, N_EDGES = 100000, 25000
S, V = 64, 32
V3 = 3 * V
D = S + V3
ROW = D + 1
TILE = P
PAIRS = -(-N_EDGES // (2 * TILE))
EDGES = PAIRS * 2 * TILE
J = 4
GROUPS = -(-N_NODES // (P * J))
NODES = GROUPS * P * J
TABLE = NODES + 2 * TILE
OUT0 = 96 + V3
OUT1 = D + 1
EPS = 1e-5


def chunks(words, least, most_words):
    return next(n for n in range(least, words + 1) if words % n == 0 and words // n <= most_words)


ZERO_W = 5600
EDGE_ROUNDS = (PAIRS - 4) // 2 - 2
ZERO_DMAS = (chunks(TABLE * OUT0 // P, 1, ZERO_W), chunks(TABLE * OUT1 // P, EDGE_ROUNDS, ZERO_W))


class Layer:

    def __init__(self, k):
        self.k = k


class Turn:

    def __init__(self, i, offset, unroll, total):
        self.i, self.offset, self.unroll, self.total = i, offset, unroll, total

    def plus(self, d):
        return Turn(self.i, self.offset + d, self.unroll, self.total)

    @property
    def n(self):
        return self.unroll * self.i + self.offset

    def slot(self, ring):
        return self.offset % ring

    @property
    def round(self):
        return self.i + self.offset // self.unroll

    @property
    def exists(self):
        return not isinstance(self.i, int) or 0 <= self.n < self.total

    def back(self, d):
        return not isinstance(self.i, int) or self.n >= d


def wait_apart(engine, sem, value):
    engine.wait_ge(sem, value)
    if not isinstance(value, int):
        engine.nop(nofuse=True)


def run_turns(engine, total, unroll, lead, tail, body):
    first = unroll * -(-4 // unroll)
    last = (total - lead) // unroll * unroll
    for s in range(-lead, first):
        body(Turn(0, s, unroll, total))
    with engine.Fori(first // unroll, last // unroll) as i:
        for s in range(unroll):
            body(Turn(i, s, unroll, total))
    for s in range(last, total + tail):
        body(Turn(0, s, unroll, total))


def build_gnn(nc, t_in, out):
    fp32 = mybir.dt.float32
    i32 = mybir.dt.int32
    ALU = mybir.AluOpType
    ACT = mybir.ActivationFunctionType
    AX = mybir.AxisListType

    sums0 = nc.dram_tensor("sums0", [TABLE, OUT0], fp32).ap()
    sums1 = nc.dram_tensor("sums1", [TABLE, OUT1], fp32).ap()
    x1_rows = nc.dram_tensor("x1_rows", [NODES, ROW], fp32).ap()
    unit_rows = nc.dram_tensor("unit_rows", [P, PAIRS * 10], fp32).ap()

    ctx = ExitStack()
    with ctx:
        def sb(name, shape, dt=fp32):
            return ctx.enter_context(nc.sbuf_tensor(name, shape, dt))

        def pb(name, shape, dt=fp32):
            return ctx.enter_context(nc.psum_tensor(name, shape, dt))

        def sem(name):
            return ctx.enter_context(nc.semaphore(name))

        def ring(name, n):
            return [sem(f"{name}_{k}") for k in range(n)]

        ident = sb("ident", [P, P])
        earlier = sb("earlier", [P, 2, 2 * TILE])
        spare_i = sb("spare_i", [P, 2], i32)
        spare = sb("spare", [P, 2])
        minus_half = sb("minus_half", [P, 2 * PAIRS])
        vec = sb("vec", [P, 2 * PAIRS, 3])
        vec_sq = sb("vec_sq", [P, 2 * PAIRS, 3])
        vec_n = sb("vec_n", [P, 2 * PAIRS])
        vec_r = sb("vec_r", [P, 2 * PAIRS])
        unit = sb("unit", [P, 2 * PAIRS, 5])
        zeros = sb("zeros", [P, ZERO_W])
        wt = {n: sb("w_" + n, list(t_in[n].shape)) for n in (
            "fc1_0", "fc2_0", "in_s_0", "in_v_0", "out_s_0", "out_a_0", "out_b_0", "out_c_0",
            "fc1_1", "fc2_1", "in_s_1", "in_v_1", "out_s_1", "out_angle_1", "out_a_1", "out_b_1",
            "skip_a_0", "skip_b_0", "skip_a_1", "skip_b_1")}
        R10, R96 = 10.0 ** -0.5, 96.0 ** -0.5
        weight_scale = {
            "out_s_0": 1 / 32, "out_a_0": 3 ** 0.5 / 32, "out_b_0": 1 / 32, "out_c_0": 1.5 ** 0.5 / 32,
            "fc2_1": 1 / 8, "in_s_1": 1 / 8, "in_v_1": 32 ** -0.5,
            "out_s_1": R10 * R96, "out_angle_1": 0.1 * R10 * R96, "out_a_1": R10 * R96, "out_b_1": R10 * R96,
            "skip_a_1": None, "skip_b_1": 32 ** -0.5}

        s_setup = sem("constants_loaded")
        s_zero_tile = sem("zero_tile_ready")
        s_zeroed0, s_zeroed1 = sem("sums0_zeroed"), sem("sums1_zeroed")
        s_pool_const = sem("pool_constants")
        s_spare = sem("spare_ready")
        s_outer_zero = sem("outer_zeroed")
        s_scaled = sem("weights_scaled")
        s_vec_sq, s_vec_n, s_vec_r, s_unit = sem("vec_squared"), sem("vec_norm"), sem("vec_inverse"), sem("unit_ready")
        s_unit_stored = sem("unit_stored")

        def edge_layer(k):
            L = Layer(k)
            L.hid_in = S if k == 0 else 8
            L.w = 224 if k == 0 else 192
            L.xv = 160 if k == 0 else V3
            L.x = S + L.xv
            L.pw = 352 if k == 0 else 256
            L.blocks = [(0, 96), (96, 64), (160, 96)] + ([(256, 96)] if k == 0 else [])
            L.out = OUT0 if k == 0 else OUT1
            L.s_out = 96 if k == 0 else S
            L.geo = 5 if k == 0 else 4
            L.hidden_dram = t_in["hidden_in_%d" % k]
            L.geo_dram = unit_rows if k == 0 else t_in["edge_y"]
            L.gather_key = t_in["dst_cols" if k == 0 else "src_cols"]
            L.key_cols = t_in["src_cols" if k == 0 else "dst_cols"]
            L.key_rows = t_in["src_rows" if k == 0 else "dst_rows"]
            L.rows = t_in["x_rows"] if k == 0 else x1_rows
            L.sums = sums0 if k == 0 else sums1
            L.zeroed = s_zeroed0 if k == 0 else s_zeroed1
            L.zero_dmas = ZERO_DMAS[k]
            n = lambda x: "%s_%d" % (x, k)
            L.hid = [sb(n("hid%d" % b), [L.hid_in, 2 * TILE]) for b in range(2)]
            L.gidx = [sb(n("gidx%d" % b), [P, 2], i32) for b in range(2)]
            L.kcol = [sb(n("kcol%d" % b), [P, 2], i32) for b in range(2)]
            L.krow = [sb(n("krow%d" % b), [P, 2 * TILE], i32) for b in range(2)]
            L.geom = [sb(n("geom%d" % b), [P, 2, L.geo]) for b in range(2)]
            L.geo_s = [sb(n("geos%d" % b), [P, 2, 4]) for b in range(2)]
            L.attr = sb(n("attr"), [P, 2])
            L.got = [sb(n("got%d" % b), [P, 2, ROW]) for b in range(2)]
            L.hT = sb(n("hT"), [S, 2 * TILE])
            L.xsT = sb(n("xsT"), [S, 2, TILE])
            L.xvT = sb(n("xvT"), [V3, 2, TILE])
            L.xs = sb(n("xs"), [P, 2, L.x])
            L.prod = sb(n("prod"), [P, 2, L.pw])
            L.t0, L.t1, L.t2 = (sb(n("t%d" % j), [P, 2, V3]) for j in range(3))
            L.dot = sb(n("dot"), [P, 2, V])
            L.cross = sb(n("cross"), [P, 2, V3])
            L.pT = sb(n("pT"), [96, 2, len(L.blocks), TILE])
            L.msg = sb(n("msg"), [P, 2, L.out])
            L.outer = sb(n("outer"), [P, 2, L.out])
            L.same = [sb(n("same%d" % b), [P, 2, 2 * TILE]) for b in range(2)]
            L.key = sb(n("key"), [P, 2])
            L.junk = sb(n("junk"), [P, 2, 2 * TILE])
            L.before = sb(n("before"), [P, 2])
            L.away = sb(n("away"), [P, 2])
            L.move = sb(n("move"), [P, 2])
            L.sidx = [sb(n("sidx%d" % b), [P, 2], i32) for b in range(2)]
            L.acc = [sb(n("acc%d" % b), [P, 2, L.out]) for b in range(2)]
            L.hidden_loaded = ring(n("hidden_loaded"), 2)
            L.gidx_loaded = ring(n("gidx_loaded"), 2)
            L.keys_loaded = ring(n("keys_loaded"), 2)
            L.geom_loaded = ring(n("geom_loaded"), 2)
            L.gathered = ring(n("gathered"), 2)
            L.scattered = ring(n("scattered"), 2)
            L.features_up = sem(n("features_up"))
            L.lhs_ready = sem(n("lhs_ready"))
            L.wx_done = sem(n("wx_done"))
            L.x_ready = sem(n("x_ready"))
            L.products_ready = sem(n("products_ready"))
            L.pt_done = sem(n("pt_done"))
            L.pt_ready = sem(n("pt_ready"))
            L.m_done = sem(n("m_done"))
            L.msg_ready = sem(n("msg_ready"))
            L.same_ready = sem(n("same_ready"))
            L.sidx_ready = sem(n("sidx_ready"))
            L.c_done = sem(n("c_done"))
            L.acc_ready = sem(n("acc_ready"))
            L.key_ready = sem(n("key_ready"))
            L.before_ready = sem(n("before_ready"))
            L.away_ready = sem(n("away_ready"))
            L.move_ready = sem(n("move_ready"))
            L.t0_ready = sem(n("t0_ready"))
            L.cross_parts = sem(n("cross_parts"))
            L.dot_ready = sem(n("dot_ready"))
            L.cross_ready = sem(n("cross_ready"))
            L.outer_ready = sem(n("outer_ready"))
            L.geo_ready = sem(n("geo_ready"))
            return L

        layers = [edge_layer(0), edge_layer(1)]

        bank = [pb("bank%d" % k, [P, 512]) for k in range(4)]
        wide = [pb("wide%d" % k, [P, 1024]) for k in range(2)]
        pH = bank[0][:, 0:2 * TILE]
        pXT = bank[1]
        pC = bank[2]
        pM = bank[3]
        pPT = wide[0]
        pW = wide[1][:, 0:512]
        pX = wide[1][:, 512:1024]

        def node_layer(k):
            L = Layer(k)
            L.sums_w = OUT0 if k == 0 else OUT1
            L.x_dram = t_in["x_rows"] if k == 0 else x1_rows
            L.sums = sums0 if k == 0 else sums1
            L.out_w = ROW if k == 0 else D
            L.out_dram = x1_rows if k == 0 else out
            n = lambda x: "%s_n%d" % (x, k)
            L.x = [sb(n("x%d" % b), [P, J, ROW]) for b in range(4)]
            L.agg = [sb(n("agg%d" % b), [P, J, L.sums_w]) for b in range(4)]
            L.tail = [sb(n("tail%d" % b), [P, J * (D - P)]) for b in range(2)]
            L.xT = [sb(n("xT%d" % b), [P, J + 1, P]) for b in range(2)]
            L.y = [sb(n("y%d" % b), [P, J, D]) for b in range(2)]
            L.gate = [sb(n("gate%d" % b), [P, J, V]) for b in range(2)]
            L.stats = sb(n("stats"), [P, J, 6])
            L.mv = [sb(n("mv%d" % b), [P, J, 2]) for b in range(2)]
            L.varp = sb(n("varp"), [P, J])
            L.rstd = [sb(n("rstd%d" % b), [P, J]) for b in range(2)]
            L.meanr = sb(n("meanr"), [P, J])
            L.shift = [sb(n("shift%d" % b), [P, J]) for b in range(2)]
            L.res = [sb(n("res%d" % b), [P, J, L.out_w]) for b in range(4)]
            L.x_loaded = ring(n("x_loaded"), 4)
            L.sums_loaded = ring(n("sums_loaded"), 4)
            L.stored = ring(n("stored"), 4)
            L.tail_ready = sem(n("tail_ready"))
            L.xt_done = sem(n("xt_done"))
            L.xt_ready = sem(n("xt_ready"))
            L.o_done = sem(n("o_done"))
            L.silu_ready = sem(n("silu_ready"))
            L.tanh_ready = sem(n("tanh_ready"))
            L.gate_ready = sem(n("gate_ready"))
            L.gated_ready = sem(n("gated_ready"))
            L.y_ready = sem(n("y_ready"))
            L.attr_copied = sem(n("attr_copied"))
            L.stats_ready = sem(n("stats_ready"))
            L.mv_ready = sem(n("mv_ready"))
            L.varp_ready = sem(n("varp_ready"))
            L.rstd_ready = sem(n("rstd_ready"))
            L.meanr_ready = sem(n("meanr_ready"))
            L.shift_ready = sem(n("shift_ready"))
            L.norm_ready = sem(n("norm_ready"))
            L.angle_step = sem(n("angle_step"))
            L.angle_ready = sem(n("angle_ready"))
            L.sin_ready = sem(n("sin_ready"))
            L.factor_step = sem(n("factor_step"))
            L.factors_ready = sem(n("factors_ready"))
            L.z1_ready = sem(n("z1_ready"))
            L.ang = [sb(n("ang%d" % j), [P, J]) for j in range(4)]
            L.red = sb(n("red"), [P, J])
            L.sin1 = sb(n("sin1"), [P, J])
            L.sin2 = sb(n("sin2"), [P, J])
            L.sq = sb(n("sq"), [P, J])
            L.cosq = sb(n("cosq"), [P, J])
            L.fcos = [sb(n("fcos%d" % b), [P, J]) for b in range(2)]
            L.fsin = [sb(n("fsin%d" % b), [P, J]) for b in range(2)]
            return L

        nodes = [node_layer(0), node_layer(1)]

        def group(dram, turn, w):
            return dram[0:NODES, :].rearrange("(g p j) w -> g p (j w)", p=P, j=J)[turn.n]

        block = ctx.enter_context(nc.Block())

        def zero_part(sp, k, i):
            w = TABLE * (OUT0, OUT1)[k] // P // ZERO_DMAS[k]
            parts = (sums0, sums1)[k].rearrange("r w -> (r w)").rearrange("(n p w) -> n p w", p=P, w=w)
            sp.dma_start(parts[i], zeros[:, 0:w]).then_inc((s_zeroed0, s_zeroed1)[k], 16)

        def sync_edges(sp, L):
            if L.k == 0:
                sp.wait_ge(s_unit_stored, 16)
                for i in range(EDGE_ROUNDS, ZERO_DMAS[1]):
                    zero_part(sp, 1, i)

            def turn(s):
                if L.k == 0 and not isinstance(s.i, int) and s.offset == 0:
                    zero_part(sp, 1, s.i - 2)
                t = s.plus(4)
                if t.exists:
                    b = t.slot(2)
                    if t.back(2):
                        sp.wait_ge(L.gathered[b], 32 * t.round)
                    sp.dma_start(L.gidx[b][:, :], L.gather_key[:, bass.ds(2 * t.n, 2)]).then_inc(L.gidx_loaded[b], 16)
                t = s.plus(3)
                if t.exists:
                    b = t.slot(2)
                    if t.back(2):
                        sp.wait_ge(L.features_up, t.n - 1)
                    sp.dma_start(L.hid[b][:, :], L.hidden_dram[:, bass.ds(2 * TILE * t.n, 2 * TILE)]).then_inc(L.hidden_loaded[b], 16)
                t = s.plus(2)
                if t.exists:
                    b = t.slot(2)
                    if t.back(2):
                        sp.wait_ge(L.same_ready, t.n - 1)
                    sp.dma_start(L.kcol[b][:, :], L.key_cols[:, bass.ds(2 * t.n, 2)]).then_inc(L.keys_loaded[b], 16)
                    sp.dma_start(L.krow[b][:, :], L.key_rows[bass.ds(t.n, 1), :].to_broadcast((P, 2 * TILE))).then_inc(L.keys_loaded[b], 16)
                    if t.back(2):
                        sp.wait_ge(L.msg_ready, t.n - 1)
                    sp.dma_start(L.geom[b][:, :, :].rearrange("p a g -> p (a g)"),
                                 L.geo_dram[:, bass.ds(2 * L.geo * t.n, 2 * L.geo)]).then_inc(L.geom_loaded[b], 16)

            run_turns(sp, PAIRS, 2, 4, 1, turn)

        def sync_nodes(sp, L):
            def turn(s):
                t = s.plus(3)
                if t.exists:
                    b = t.slot(4)
                    if t.back(4):
                        sp.wait_ge(L.y_ready, t.n - 3)
                        sp.wait_ge(L.o_done, t.n - 3)
                        if L.k == 0:
                            sp.wait_ge(L.attr_copied, t.n - 3)
                    sp.dma_start(L.x[b][:, :, :].rearrange("p j w -> p (j w)"), group(L.x_dram, t, ROW)).then_inc(L.x_loaded[b], 16)
                    sp.dma_start(L.agg[b][:, :, :].rearrange("p j w -> p (j w)"), group(L.sums, t, L.sums_w)).then_inc(L.sums_loaded[b], 16)
                t = s.plus(-2)
                if t.exists:
                    b = t.slot(4)
                    sp.wait_ge(L.norm_ready, t.n + 1)
                    if L.k == 0:
                        sp.wait_ge(L.attr_copied, t.n + 1)
                    sp.dma_start(group(L.out_dram, t, L.out_w), L.res[b][:, :, :].rearrange("p j w -> p (j w)")).then_inc(L.stored[b], 16)

            run_turns(sp, GROUPS, 4, 3, 2, turn)

        @block.sync
        def _(sp):
            sp.dma_start(vec[:, :, :].rearrange("p t c -> p (t c)"), t_in["edge_vec"]).then_inc(s_setup, 16)
            for n in wt:
                sp.dma_start(wt[n][:, :], t_in[n]).then_inc(s_setup, 16)
            sp.wait_ge(s_zero_tile, 1)
            with sp.Fori(0, ZERO_DMAS[0]) as i:
                zero_part(sp, 0, i)
            sp.wait_ge(s_unit, 1)
            sp.dma_start(unit_rows, unit[:, :, :].rearrange("p t c -> p (t c)")).then_inc(s_unit_stored, 16)
            sync_edges(sp, layers[0])
            for b in range(2):
                sp.wait_ge(layers[0].scattered[b], 32 * (PAIRS // 2))
            sync_nodes(sp, nodes[0])
            for b in range(4):
                sp.wait_ge(nodes[0].stored[b], 16 * (GROUPS // 4))
            sync_edges(sp, layers[1])
            for b in range(2):
                sp.wait_ge(layers[1].scattered[b], 32 * (PAIRS // 2))
            sync_nodes(sp, nodes[1])
            for b in range(4):
                sp.wait_ge(nodes[1].stored[b], 16 * (GROUPS // 4))

        def pool_edges(pool, L):
            def turn(s):
                t = s.plus(3)
                if t.exists:
                    b = t.slot(2)
                    if t.back(2):
                        pool.wait_ge(L.features_up, t.n - 1)
                        if L.k == 1:
                            pool.wait_ge(L.lhs_ready, t.n - 1)
                    wait_apart(pool, L.gidx_loaded[b], 16 * (t.round + 1))
                    for a in range(2):
                        nc.gpsimd.indirect_dma_start(
                            L.got[b][:, a, :], None, L.rows, bass.IndirectOffsetOnAxis(ap=L.gidx[b][:, a:a + 1], axis=0)
                        ).then_inc(L.gathered[b], 16)
                t = s.plus(-1)
                if t.exists:
                    b = t.slot(2)
                    pool.wait_ge(L.acc_ready, t.n + 1)
                    pool.wait_ge(L.sidx_ready, t.n + 1)
                    if t.back(1):
                        u = t.plus(-1)
                        wait_apart(pool, L.scattered[u.slot(2)], 32 * (u.round + 1))
                    else:
                        pool.wait_ge(L.zeroed, 16 * L.zero_dmas)
                    for a in range(2):
                        nc.gpsimd.indirect_dma_start(
                            L.sums, bass.IndirectOffsetOnAxis(ap=L.sidx[b][:, a:a + 1], axis=0), L.acc[b][:, a, :], None,
                            bounds_check=TABLE - 1, oob_is_err=True, compute_op=ALU.add,
                        ).then_inc(L.scattered[b], 16)

            run_turns(pool, PAIRS, 2, 4, 1, turn)

        def pool_norm(pool, L, t):
            b = t.slot(2)
            wait_apart(pool, L.mv_ready, t.n + 1)
            nc.gpsimd.tensor_scalar(L.varp[:, :], L.mv[b][:, :, 1], EPS, None, ALU.add).then_inc(L.varp_ready, 1)
            pool.wait_ge(L.varp_ready, t.n + 1)
            if t.back(2):
                pool.wait_ge(L.norm_ready, t.n - 1)
            nc.gpsimd.tensor_tensor(L.rstd[b][:, :], L.varp[:, :], minus_half[:, 0:J], ALU.pow).then_inc(L.rstd_ready, 1)
            pool.wait_ge(L.rstd_ready, t.n + 1)
            nc.gpsimd.tensor_tensor(L.meanr[:, :], L.mv[b][:, :, 0], L.rstd[b][:, :], ALU.mult).then_inc(L.meanr_ready, 1)
            wait_apart(pool, L.meanr_ready, t.n + 1)
            nc.gpsimd.tensor_scalar(L.shift[b][:, :], L.meanr[:, :], -1.0, None, ALU.mult).then_inc(L.shift_ready, 1)

        def pool_tail(pool, L, t):
            b, b4 = t.slot(2), t.slot(4)
            if t.back(2):
                pool.wait_ge(L.xt_done, t.n - 1)
            wait_apart(pool, L.x_loaded[b4], 16 * (t.round + 1))
            nc.gpsimd.tensor_copy(L.tail[b][:, :].rearrange("p (j c) -> p j c", c=D - P), L.x[b4][:, :, P:D]).then_inc(L.tail_ready, 1)

        def pool_nodes0(pool, L):
            def turn(s):
                t = s.plus(-1)
                if t.exists:
                    pool_norm(pool, L, t)
                t = s
                if t.exists:
                    b = t.slot(2)
                    if t.back(4):
                        pool.wait_ge(L.stored[t.slot(4)], 16 * t.round)
                    wait_apart(pool, L.x_loaded[t.slot(4)], 16 * (t.round + 1))
                    nc.gpsimd.tensor_copy(L.res[t.slot(4)][:, :, D:ROW], L.x[t.slot(4)][:, :, D:ROW]).then_inc(L.attr_copied, 1)
                    pool.wait_ge(L.silu_ready, t.n + 1)
                    pool.wait_ge(L.gated_ready, t.n + 1)
                    nc.gpsimd.tensor_tensor(L.y[b][:, :, :], L.y[b][:, :, :], L.x[t.slot(4)][:, :, 0:D], ALU.add).then_inc(L.y_ready, 1)
                t = s.plus(2)
                if t.exists:
                    pool_tail(pool, L, t)

            run_turns(pool, GROUPS, 4, 3, 2, turn)

        TWO_PI = [6.28125, 0.0019350051879882812, 3.0199159819567e-07]
        ROUNDER = 12582912.0
        ANGLE_STEPS, FACTOR_STEPS = 9, 3

        def pool_nodes1(pool, L):
            gp = nc.gpsimd

            def angles(t):
                b4 = t.slot(4)
                done = [0]

                def step(ins):
                    done[0] += 1
                    ins.then_inc(L.angle_step, 1)
                    wait_apart(pool, L.angle_step, ANGLE_STEPS * t.n + done[0])

                a, k, m, r = (x[:, :] for x in L.ang)
                pool.wait_ge(L.x_loaded[b4], 16 * (t.round + 1))
                pool.wait_ge(L.sums_loaded[b4], 16 * (t.round + 1))
                step(gp.tensor_tensor(a, L.agg[b4][:, :, D], L.x[b4][:, :, D], ALU.mult))
                step(gp.tensor_scalar(k, a, 0.15915494309189535, ROUNDER, ALU.mult, ALU.add))
                step(gp.tensor_scalar(k, k, ROUNDER, None, ALU.subtract))
                cur = a
                for part in TWO_PI:
                    step(gp.tensor_scalar(m, k, part, None, ALU.mult))
                    step(gp.tensor_tensor(r, cur, m, ALU.subtract))
                    cur = r
                if t.back(1):
                    wait_apart(pool, L.sin_ready, t.n)
                gp.tensor_scalar(L.red[:, :], r, 3.1415925, -3.1415925, ALU.min, ALU.max).then_inc(L.angle_ready, 1)

            def factors(t):
                b, b4 = t.slot(2), t.slot(4)
                done = [0]

                def step(ins):
                    done[0] += 1
                    ins.then_inc(L.factor_step, 1)
                    wait_apart(pool, L.factor_step, FACTOR_STEPS * t.n + done[0])

                pool.wait_ge(L.sin_ready, t.n + 1)
                attr = L.x[b4][:, :, D]
                step(gp.tensor_tensor(L.sq[:, :], L.sin2[:, :], L.sin2[:, :], ALU.mult))
                step(gp.tensor_scalar(L.cosq[:, :], L.sq[:, :], -2.0, 1.0, ALU.mult, ALU.add))
                if t.back(2):
                    pool.wait_ge(L.y_ready, t.n - 1)
                step(gp.tensor_tensor(L.fcos[b][:, :], L.cosq[:, :], attr, ALU.mult))
                gp.tensor_tensor(L.fsin[b][:, :], L.sin1[:, :], attr, ALU.mult).then_inc(L.factors_ready, 1)

            def turn(s):
                t = s.plus(1)
                if t.exists:
                    angles(t)
                t = s.plus(-1)
                if t.exists:
                    pool_norm(pool, L, t)
                t = s.plus(1)
                if t.exists:
                    factors(t)
                t = s.plus(2)
                if t.exists:
                    pool_tail(pool, L, t)

            run_turns(pool, GROUPS, 4, 3, 2, turn)

        @block.gpsimd
        def _(pool):
            gp = nc.gpsimd
            gp.memset(zeros[:, :], 0.0).then_inc(s_zero_tile, 1)
            gp.memset(minus_half[:, :], -0.5)
            gp.memset(ident[:, :], 0.0).then_inc(s_pool_const, 1)
            gp.memset(earlier[:, :, :], 1.0).then_inc(s_pool_const, 1)
            pool.wait_ge(s_pool_const, 2)
            gp.affine_select(out=ident[:, :], in_=ident[:, :], compare_op=ALU.not_equal, fill=1.0, base=0,
                             pattern=[[-1, P]], channel_multiplier=1).then_inc(s_pool_const, 1)
            for a in range(2):
                gp.affine_select(out=earlier[:, a, :], in_=earlier[:, a, :], compare_op=ALU.is_gt, fill=0.0, base=TILE * a,
                                 pattern=[[-1, 2 * TILE]], channel_multiplier=1).then_inc(s_pool_const, 1)
            gp.iota(spare_i[:, :], pattern=[[TILE, 2]], base=NODES, channel_multiplier=1).then_inc(s_spare, 1)
            pool.wait_ge(s_spare, 1)
            gp.tensor_copy(spare[:, :], spare_i[:, :]).then_inc(s_pool_const, 1)
            pool.wait_ge(s_pool_const, 6)
            pool.wait_ge(s_vec_n, 1)
            gp.tensor_tensor(vec_r[:, :], vec_n[:, :], minus_half[:, :], ALU.pow).then_inc(s_vec_r, 1)
            pool_edges(pool, layers[0])
            pool_nodes0(pool, nodes[0])
            for b in range(4):
                pool.wait_ge(nodes[0].stored[b], 16 * (GROUPS // 4))
            pool_edges(pool, layers[1])
            pool_nodes1(pool, nodes[1])

        def pe_edges(pe, L):
            mm = nc.tensor.matmul
            fc1, fc2 = wt["fc1_%d" % L.k], wt["fc2_%d" % L.k]
            in_s, in_v = wt["in_s_%d" % L.k], wt["in_v_%d" % L.k]
            W = pW[:, 0:2 * L.w].rearrange("p (a w) -> p a w", a=2)
            X = pX[:, 0:2 * L.x].rearrange("p (a w) -> p a w", a=2)
            nb = len(L.blocks)
            PT = pPT[:, 0:2 * 512].rearrange("p (a n e) -> p a n e", a=2, e=TILE)
            M = pM[:, 0:448].rearrange("p (a w) -> p a w", a=2)
            C = pC[:, 0:2 * L.out].rearrange("p (a w) -> p a w", a=2)

            def turn(s):
                t = s.plus(1)
                if t.exists:
                    pe.wait_ge(L.lhs_ready, t.n + 1)
                    if t.back(1):
                        pe.wait_ge(L.products_ready, t.n)
                    for a in range(2):
                        e = bass.ds(a * TILE, TILE)
                        mm(W[:, a, :], L.hT[:, e], fc2[:, :], start=True, stop=True)
                        mm(X[:, a, 0:S], L.xsT[:, a, :], in_s[:, :], start=True, stop=True)
                        last = mm(X[:, a, S:L.x], L.xvT[:, a, :], in_v[:, :], start=True, stop=True)
                    last.then_inc(L.wx_done, 1)
                t = s.plus(-1)
                if t.exists:
                    b = t.slot(2)
                    pe.wait_ge(L.msg_ready, t.n + 1)
                    pe.wait_ge(L.same_ready, t.n + 1)
                    if t.back(1):
                        pe.wait_ge(L.acc_ready, t.n)
                    for j in range(2):
                        for a in range(2):
                            last = mm(C[:, j, :], L.same[b][:, a, j * TILE:(j + 1) * TILE], L.msg[:, a, :],
                                      start=(a == 0), stop=(a == 1))
                    last.then_inc(L.c_done, 1)
                t = s
                if t.exists:
                    pe.wait_ge(L.products_ready, t.n + 1)
                    if t.back(1):
                        pe.wait_ge(L.pt_ready, t.n)
                    for a in range(2):
                        for n, (c, w) in enumerate(L.blocks):
                            last = nc.tensor.transpose(PT[0:w, a, n, :], L.prod[:, a, c:c + w], ident[:, :])
                    last.then_inc(L.pt_done, 1)
                t = s.plus(2)
                if t.exists:
                    b = t.slot(2)
                    if t.back(1):
                        pe.wait_ge(L.lhs_ready, t.n)
                    pe.wait_ge(L.gathered[b], 32 * (t.round + 1))
                    wait_apart(pe, L.hidden_loaded[b], 16 * (t.round + 1))
                    mm(pH[0:S, :], fc1[:, :], L.hid[b][:, :], start=True, stop=True)
                    for a in range(2):
                        nc.tensor.transpose(pXT[0:S, a * TILE:(a + 1) * TILE], L.got[b][:, a, 0:S], ident[:, :])
                        last = nc.tensor.transpose(pXT[0:V3, (2 + a) * TILE:(3 + a) * TILE], L.got[b][:, a, S:D], ident[:, :])
                    last.then_inc(L.features_up, 1)
                t = s
                if t.exists:
                    pe.wait_ge(L.pt_ready, t.n + 1)
                    if t.back(1):
                        pe.wait_ge(L.msg_ready, t.n)
                    so = L.s_out
                    for a in range(2):
                        last = mm(M[:, a, 0:so], L.pT[:, a, 0, :], wt["out_s_%d" % L.k][:, :], start=True, stop=True)
                        if L.k == 0:
                            mm(M[:, a, 96:192], L.pT[:, a, 2, :], wt["out_b_0"][:, :], start=True, stop=False)
                            mm(M[:, a, 96:192], L.pT[:, a, 3, :], wt["out_c_0"][:, :], start=False, stop=True)
                            last = mm(M[:, a, 192:224], L.pT[0:S, a, 1, :], wt["out_a_0"][:, :], start=True, stop=True)
                        else:
                            mm(M[:, a, 160:161], L.pT[:, a, 0, :], wt["out_angle_1"][:, :], start=True, stop=True)
                            mm(M[:, a, 64:160], L.pT[:, a, 2, :], wt["out_b_1"][:, :], start=True, stop=True)
                            last = mm(M[:, a, 192:224], L.pT[0:S, a, 1, :], wt["out_a_1"][:, :], start=True, stop=True)
                    last.then_inc(L.m_done, 1)

            run_turns(pe, PAIRS, 2, 4, 1, turn)

        xt_psum = [wide[0], wide[1]]
        o_psum = [[bank[0], bank[1]], [bank[2], bank[3]]]

        def pe_nodes(pe, L):
            mm = nc.tensor.matmul
            wa, wb = wt["skip_a_%d" % L.k], wt["skip_b_%d" % L.k]
            w = 192 if L.k == 0 else D

            def turn(s):
                t = s.plus(1)
                if t.exists:
                    b = t.slot(2)
                    x = L.x[t.slot(4)]
                    xt = xt_psum[b]
                    pe.wait_ge(L.x_loaded[t.slot(4)], 16 * (t.round + 1))
                    if t.back(2):
                        pe.wait_ge(L.xt_ready, t.n - 1)
                    for j in range(J):
                        nc.tensor.transpose(xt[:, j * P:(j + 1) * P], x[:, j, 0:P], ident[:, :])
                    pe.wait_ge(L.tail_ready, t.n + 1)
                    nc.tensor.transpose(xt[:, J * P:(J + 1) * P], L.tail[b][:, :], ident[:, :]).then_inc(L.xt_done, 1)
                t = s
                if t.exists:
                    b = t.slot(2)
                    pe.wait_ge(L.xt_ready, t.n + 1)
                    if L.k == 0:
                        pe.wait_ge(L.sums_loaded[t.slot(4)], 16 * (t.round + 1))
                    if t.back(2):
                        if L.k == 0:
                            pe.wait_ge(L.tanh_ready, t.n - 1)
                            pe.wait_ge(L.gated_ready, t.n - 1)
                        else:
                            pe.wait_ge(L.y_ready, t.n - 1)
                    for j in range(J):
                        o = o_psum[b][j // 2][:, (j % 2) * 256:(j % 2) * 256 + w]
                        if L.k == 0:
                            mm(o, ident[:, :], L.agg[t.slot(4)][:, j, :], start=True, stop=False)
                            mm(o, L.xT[b][:, j, :], wa[:, :], start=False, stop=False)
                            last = mm(o, L.xT[b][:, J, :], wb[:, j * w:(j + 1) * w], start=False, stop=True)
                        else:
                            mm(o, L.xT[b][:, j, :], wa[:, :], start=True, stop=False)
                            last = mm(o, L.xT[b][:, J, :], wb[:, j * w:(j + 1) * w], start=False, stop=True)
                    last.then_inc(L.o_done, 1)

            run_turns(pe, GROUPS, 4, 3, 2, turn)

        @block.tensor
        def _(pe):
            pe.wait_ge(s_pool_const, 6)
            pe.wait_ge(s_scaled, 1)
            pe_edges(pe, layers[0])
            pe_nodes(pe, nodes[0])
            pe_edges(pe, layers[1])
            pe_nodes(pe, nodes[1])

        def act_edges(act, L):
            nb = len(L.blocks)
            X = pX[:, 0:2 * L.x]
            PT = pPT[:, 0:2 * 512].rearrange("p (a n e) -> p a (n e)", a=2, e=TILE)
            M = pM[:, 0:448].rearrange("p (a w) -> p a w", a=2)
            copy, cp = nc.scalar.activation, ACT.Copy

            def turn(s):
                t = s.plus(1)
                if t.exists:
                    act.wait_ge(L.wx_done, t.n + 1)
                    if t.back(1):
                        act.wait_ge(L.products_ready, t.n)
                    copy(L.xs[:, :, :].rearrange("p a w -> p (a w)"), X, cp).then_inc(L.x_ready, 1)
                t = s.plus(-1)
                if t.exists:
                    b = t.slot(2)
                    act.wait_ge(L.c_done, t.n + 1)
                    if t.back(2):
                        act.wait_ge(L.scattered[b], 32 * t.round)
                    copy(L.acc[b][:, :, :].rearrange("p a w -> p (a w)"), pC[:, 0:2 * L.out], cp).then_inc(L.acc_ready, 1)
                t = s
                if t.exists:
                    act.wait_ge(L.pt_done, t.n + 1)
                    if t.back(1):
                        act.wait_ge(L.m_done, t.n)
                    for lo, hi, rows in ((0, 1, 96), (1, 2, S), (2, nb, 96)):
                        last = copy(L.pT[0:rows, :, lo:hi, :].rearrange("p a n e -> p a (n e)"),
                                    PT[0:rows, :, lo * TILE:hi * TILE], cp)
                    last.then_inc(L.pt_ready, 1)
                t = s.plus(2)
                if t.exists:
                    b = t.slot(2)
                    act.wait_ge(L.features_up, t.n + 1)
                    if t.back(1):
                        act.wait_ge(L.wx_done, t.n)
                    if L.k == 0:
                        copy(L.hT[:, :], pH[0:S, :], ACT.Relu)
                    else:
                        copy(L.hT[:, :], pH[0:S, :], ACT.Silu, scale=8.0 ** -0.5)
                        if t.back(1):
                            act.wait_ge(L.geo_ready, t.n)
                        copy(L.attr[:, :], L.got[b][:, :, D], cp)
                    copy(L.xsT[:, :, :].rearrange("p a e -> p (a e)"), pXT[0:S, 0:2 * TILE], cp)
                    copy(L.xvT[:, :, :].rearrange("p a e -> p (a e)"), pXT[0:V3, 2 * TILE:4 * TILE], cp).then_inc(L.lhs_ready, 1)

            run_turns(act, PAIRS, 2, 4, 1, turn)

        def act_nodes(act, L):
            f = nc.scalar.activation

            def turn(s):
                t = s.plus(1)
                if t.exists:
                    b = t.slot(2)
                    act.wait_ge(L.xt_done, t.n + 1)
                    if t.back(2):
                        act.wait_ge(L.o_done, t.n - 1)
                    xT = L.xT[b][:, :, :].rearrange("p n e -> p (n e)")
                    f(xT[:, 0:512], xt_psum[b][:, 0:512], ACT.Copy)
                    f(xT[:, 512:640], xt_psum[b][:, 512:640], ACT.Copy).then_inc(L.xt_ready, 1)
                if L.k == 1:
                    t = s.plus(1)
                    if t.exists:
                        act.wait_ge(L.angle_ready, t.n + 1)
                        if t.back(1):
                            act.wait_ge(L.factors_ready, t.n)
                        f(L.sin1[:, :], L.red[:, :], ACT.Sin)
                        f(L.sin2[:, :], L.red[:, :], ACT.Sin, scale=0.5).then_inc(L.sin_ready, 1)
                t = s
                if t.exists and L.k == 0:
                    b = t.slot(2)
                    act.wait_ge(L.o_done, t.n + 1)
                    if t.back(2):
                        act.wait_ge(L.norm_ready, t.n - 1)
                    for h in range(2):
                        o = o_psum[b][h][:, :].rearrange("p (j w) -> p j w", w=256)
                        last = f(L.y[b][:, 2 * h:2 * h + 2, 0:S], o[:, :, 0:S], ACT.Silu)
                    last.then_inc(L.silu_ready, 1)
                    if t.back(2):
                        act.wait_ge(L.gated_ready, t.n - 1)
                    for h in range(2):
                        o = o_psum[b][h][:, :].rearrange("p (j w) -> p j w", w=256)
                        last = f(L.gate[b][:, 2 * h:2 * h + 2, :], o[:, :, S:96], ACT.Tanh, scale=0.5)
                    last.then_inc(L.tanh_ready, 1)
                t = s.plus(-1)
                if t.exists:
                    b = t.slot(2)
                    act.wait_ge(L.shift_ready, t.n + 1)
                    if t.back(4):
                        act.wait_ge(L.stored[t.slot(4)], 16 * t.round)
                    for j in range(J):
                        last = f(L.res[t.slot(4)][:, j, 0:D], L.y[b][:, j, :], ACT.Identity,
                                 bias=L.shift[b][:, j:j + 1], scale=L.rstd[b][:, j:j + 1])
                    last.then_inc(L.norm_ready, 1)

            run_turns(act, GROUPS, 4, 3, 2, turn)

        @block.scalar
        def _(act):
            act.wait_ge(s_setup, 16 * (1 + len(wt)))
            for n, c in weight_scale.items():
                if n == "skip_a_1":
                    nc.scalar.activation(wt[n][0:S, :], wt[n][0:S, :], ACT.Copy, scale=1 / 8)
                    last = nc.scalar.activation(wt[n][S:P, :], wt[n][S:P, :], ACT.Copy, scale=32 ** -0.5)
                else:
                    last = nc.scalar.activation(wt[n][:, :], wt[n][:, :], ACT.Copy, scale=float(c))
            act.drain()
            last = nc.scalar.activation(wt["fc2_1"][:, 160:192], wt["fc2_1"][:, 160:192], ACT.Copy, scale=3 ** -0.5)
            last.then_inc(s_scaled, 1)
            act_edges(act, layers[0])
            act_nodes(act, nodes[0])
            act_edges(act, layers[1])
            act_nodes(act, nodes[1])

        def dve_edges(dve, L):
            v = nc.vector
            W = pW[:, 0:2 * L.w].rearrange("p (a w) -> p a w", a=2)
            M = pM[:, 0:448].rearrange("p (a w) -> p a w", a=2)
            vo = 96 if L.k == 0 else S

            def vec3(x):
                return x.rearrange("p a (m c) -> p a m c", c=3)

            def over3(x):
                return x.unsqueeze(3).to_broadcast((P, 2, V, 3))

            def geo(g, c):
                return g[:, :, c:c + 3].unsqueeze(2).to_broadcast((P, 2, V, 3))

            def turn(s):
                t = s
                if t.exists:
                    b = t.slot(2)
                    dve.wait_ge(L.keys_loaded[b], 32 * (t.round + 1))
                    v.tensor_copy(L.key[:, :], L.kcol[b][:, :]).then_inc(L.key_ready, 1)
                    dve.wait_ge(L.key_ready, t.n + 1)
                    for a in range(2):
                        last = v.scalar_tensor_tensor(L.junk[:, a, :], L.krow[b][:, :], L.key[:, a:a + 1], earlier[:, a, :],
                                                      ALU.is_equal, ALU.mult, accum_out=L.before[:, a:a + 1])
                    last.then_inc(L.before_ready, 1)
                    v.tensor_tensor(L.away[:, :], spare[:, :], L.key[:, :], ALU.subtract).then_inc(L.away_ready, 1)
                    if t.back(2):
                        dve.wait_ge(L.c_done, t.n - 1)
                    for a in range(2):
                        last = v.tensor_scalar(L.same[b][:, a, :], L.krow[b][:, :], L.key[:, a:a + 1], None, ALU.is_equal)
                        if a == 0:
                            dve.wait_ge(L.before_ready, t.n + 1)
                            dve.wait_ge(L.away_ready, t.n + 1)
                            v.scalar_tensor_tensor(L.move[:, :], L.before[:, :], 1.0, L.away[:, :], ALU.min, ALU.mult).then_inc(L.move_ready, 1)
                    last.then_inc(L.same_ready, 1)
                    dve.wait_ge(L.move_ready, t.n + 1)
                    if t.back(2):
                        dve.wait_ge(L.scattered[b], 32 * t.round)
                    v.tensor_tensor(L.sidx[b][:, :], L.move[:, :], L.key[:, :], ALU.add).then_inc(L.sidx_ready, 1)
                t = s.plus(1)
                if t.exists:
                    b = t.slot(2)
                    dve.wait_ge(L.geom_loaded[b], 16 * (t.round + 1))
                    if L.k == 1:
                        dve.wait_ge(L.lhs_ready, t.n + 1)
                        v.tensor_tensor(L.geo_s[b][:, :, :], L.geom[b][:, :, :],
                                        L.attr[:, :].unsqueeze(2).to_broadcast((P, 2, 4)), ALU.mult).then_inc(L.geo_ready, 1)
                        dve.wait_ge(L.geo_ready, t.n + 1)
                    dve.wait_ge(L.x_ready, t.n + 1)
                    if t.back(1):
                        dve.wait_ge(L.pt_done, t.n)
                    xs = L.xs[:, :, 0:S]
                    g = L.geom[b] if L.k == 0 else L.geo_s[b]
                    if L.k == 0:
                        xv = L.xs[:, :, S:S + 160].rearrange("p a (m c) -> p a m c", c=5)
                        v.tensor_tensor(vec3(L.t0[:, :, :]), xv[:, :, :, 0:3], geo(g, 0), ALU.mult).then_inc(L.t0_ready, 1)
                        v.tensor_tensor(vec3(L.t1[:, :, :]), xv[:, :, :, 1:4], geo(g, 2), ALU.mult)
                        v.tensor_tensor(vec3(L.t2[:, :, :]), xv[:, :, :, 2:5], geo(g, 1), ALU.mult).then_inc(L.cross_parts, 1)
                        dve.wait_ge(L.t0_ready, t.n + 1)
                        v.tensor_reduce(L.dot[:, :, :], vec3(L.t0[:, :, :]), AX.X, ALU.add).then_inc(L.dot_ready, 1)
                        dve.wait_ge(L.cross_parts, t.n + 1)
                        v.tensor_tensor(L.cross[:, :, :], L.t1[:, :, :], L.t2[:, :, :], ALU.subtract).then_inc(L.cross_ready, 1)
                        ac = L.prod[:, :, 0:192].rearrange("p a (n c) -> p a n c", c=96)[:, :, :, 0:S]
                        v.tensor_tensor(ac, W[:, :, 0:2 * S].rearrange("p a (n c) -> p a n c", c=S),
                                        xs.unsqueeze(2).to_broadcast((P, 2, 2, S)), ALU.mult)
                        v.tensor_tensor(vec3(L.prod[:, :, 160:256]), over3(W[:, :, 128:160]), xv[:, :, :, 0:3], ALU.mult)
                        dve.wait_ge(L.dot_ready, t.n + 1)
                        v.tensor_tensor(L.prod[:, :, S:96], W[:, :, 160:192], L.dot[:, :, :], ALU.mult)
                        dve.wait_ge(L.cross_ready, t.n + 1)
                        v.tensor_tensor(vec3(L.prod[:, :, 256:352]), over3(W[:, :, 192:224]), vec3(L.cross[:, :, :]),
                                        ALU.mult).then_inc(L.products_ready, 1)
                    else:
                        xv = vec3(L.xs[:, :, S:D])
                        v.tensor_tensor(vec3(L.t0[:, :, :]), xv, geo(g, 1), ALU.mult).then_inc(L.t0_ready, 1)
                        for a in range(2):
                            v.scalar_tensor_tensor(L.prod[:, a, 0:S], W[:, a, 0:S], g[:, a, 0:1], xs[:, a, :], ALU.mult, ALU.mult)
                            v.scalar_tensor_tensor(vec3(L.prod[:, :, 160:256])[:, a], W[:, a, 128:160].unsqueeze(2).to_broadcast((P, V, 3)),
                                                   g[:, a, 0:1], xv[:, a], ALU.mult, ALU.mult)
                        dve.wait_ge(L.t0_ready, t.n + 1)
                        v.tensor_reduce(L.dot[:, :, :], vec3(L.t0[:, :, :]), AX.X, ALU.add).then_inc(L.dot_ready, 1)
                        v.tensor_tensor(L.prod[:, :, 96:160], W[:, :, S:2 * S], xs, ALU.mult)
                        dve.wait_ge(L.dot_ready, t.n + 1)
                        v.tensor_tensor(L.prod[:, :, S:96], W[:, :, 160:192], L.dot[:, :, :], ALU.mult).then_inc(L.products_ready, 1)
                t = s
                if t.exists:
                    b = t.slot(2)
                    g, c = (L.geom[b], 0) if L.k == 0 else (L.geo_s[b], 1)
                    dve.wait_ge(L.m_done, t.n + 1)
                    v.tensor_tensor(vec3(L.outer[:, :, vo:vo + V3]), over3(M[:, :, 192:224]), geo(g, c), ALU.mult).then_inc(L.outer_ready, 1)
                    dve.wait_ge(L.outer_ready, t.n + 1)
                    if t.back(1):
                        dve.wait_ge(L.c_done, t.n)
                    v.tensor_tensor(L.msg[:, :, :], M[:, :, 0:L.out], L.outer[:, :, :], ALU.add).then_inc(L.msg_ready, 1)

            run_turns(dve, PAIRS, 2, 4, 1, turn)

        def dve_stats(dve, L, t):
            v = nc.vector
            b = t.slot(2)
            for j in range(J):
                last = v.bn_stats(L.stats[:, j, :], L.y[b][:, j, :])
            last.then_inc(L.stats_ready, 1)
            if t.back(2):
                dve.wait_ge(L.meanr_ready, t.n - 1)
            wait_apart(dve, L.stats_ready, t.n + 1)
            for j in range(J):
                last = v.bn_aggr(L.mv[b][:, j, :], L.stats[:, j, :])
            last.then_inc(L.mv_ready, 1)

        def dve_nodes0(dve, L):
            v = nc.vector

            def turn(s):
                t = s.plus(-1)
                if t.exists:
                    dve.wait_ge(L.y_ready, t.n + 1)
                    dve_stats(dve, L, t)
                t = s
                if t.exists:
                    b = t.slot(2)
                    dve.wait_ge(L.tanh_ready, t.n + 1)
                    v.tensor_scalar(L.gate[b][:, :, :], L.gate[b][:, :, :], 0.5, 0.5, ALU.mult, ALU.add).then_inc(L.gate_ready, 1)
                    dve.wait_ge(L.gate_ready, t.n + 1)
                    for h in range(2):
                        o = o_psum[b][h][:, :].rearrange("p (j w) -> p j w", w=256)[:, :, 96:192]
                        y = L.y[b][:, 2 * h:2 * h + 2, S:D]
                        last = v.tensor_tensor(y.rearrange("p j (m c) -> p j m c", c=3), o.rearrange("p j (m c) -> p j m c", c=3),
                                               L.gate[b][:, 2 * h:2 * h + 2, :].unsqueeze(3).to_broadcast((P, 2, V, 3)), ALU.mult)
                    last.then_inc(L.gated_ready, 1)

            run_turns(dve, GROUPS, 4, 3, 2, turn)

        def dve_nodes1(dve, L):
            v = nc.vector

            def turn(s):
                t = s
                if t.exists:
                    b, b4 = t.slot(2), t.slot(4)
                    dve.wait_ge(L.o_done, t.n + 1)
                    dve.wait_ge(L.factors_ready, t.n + 1)
                    if t.back(2):
                        dve.wait_ge(L.norm_ready, t.n - 1)
                    for j in range(J):
                        o = o_psum[b][j // 2][:, (j % 2) * 256:(j % 2) * 256 + D]
                        last = v.scalar_tensor_tensor(L.y[b][:, j, :], o, L.fcos[b][:, j:j + 1], L.x[b4][:, j, 0:D], ALU.mult, ALU.add)
                    last.then_inc(L.z1_ready, 1)
                    dve.wait_ge(L.z1_ready, t.n + 1)
                    for j in range(J):
                        last = v.scalar_tensor_tensor(L.y[b][:, j, :], L.agg[b4][:, j, 0:D], L.fsin[b][:, j:j + 1], L.y[b][:, j, :],
                                                      ALU.mult, ALU.add)
                    last.then_inc(L.y_ready, 1)
                    dve.wait_ge(L.y_ready, t.n + 1)
                    dve_stats(dve, L, t)

            run_turns(dve, GROUPS, 4, 3, 2, turn)

        @block.vector
        def _(dve):
            v = nc.vector
            dve.wait_ge(s_setup, 16 * (1 + len(wt)))
            v.tensor_tensor(vec_sq[:, :, :], vec[:, :, :], vec[:, :, :], ALU.mult).then_inc(s_vec_sq, 1)
            dve.wait_ge(s_vec_sq, 1)
            v.tensor_reduce(vec_n[:, :], vec_sq[:, :, :], AX.X, ALU.add).then_inc(s_vec_n, 1)
            dve.wait_ge(s_vec_r, 1)
            for lo, n in ((0, 3), (3, 2)):
                last = v.tensor_tensor(unit[:, :, lo:lo + n], vec[:, :, 0:n],
                                       vec_r[:, :].unsqueeze(2).to_broadcast((P, 2 * PAIRS, n)), ALU.mult)
            last.then_inc(s_unit, 1)
            dve.wait_ge(s_pool_const, 6)
            for L in layers:
                last = v.memset(L.outer[:, :, :], 0.0)
            last.then_inc(s_outer_zero, 1)
            dve.wait_ge(s_outer_zero, 1)
            dve_edges(dve, layers[0])
            dve_nodes0(dve, nodes[0])
            dve_edges(dve, layers[1])
            dve_nodes1(dve, nodes[1])


def kernel(x, src, dst, edge_attr_3, edge_attr_4, edge_attr_64, edge_attr_8, node_vec1, L0_gnn_W_skip0, L0_gnn_W_skip1,
           L0_gnn_W_nl0, L0_gnn_W_nl1, L0_gnn_W_fc1, L0_gnn_W_fc2, L0_gnn_W_out_s, L0_gnn_W_out_v, L1_gnn_W_sc_s,
           L1_gnn_W_sc_v, L1_gnn_W1_s, L1_gnn_W1_v, L1_gnn_W2_s, L1_gnn_W2_v, L1_gnn_W3, L1_gnn_fcW1, L1_gnn_fcW2):
    import numpy as np
    import concourse.bacc as bacc
    from concourse import mybir as mb
    from concourse.bass_utils import run_bass_kernel_spmd

    f32 = np.float32

    def spread(w, width=3):
        w = np.asarray(w)
        m, k = w.shape
        a = np.zeros((m, 3, k, width), f32)
        for c in range(width):
            a[:, c % 3, :, c] = w
        return a.reshape(3 * m, width * k)

    def beside(ws, wv):
        ws, wv = np.asarray(ws), spread(wv)
        a = np.zeros((D, ws.shape[1] + wv.shape[1]), f32)
        a[:S, :ws.shape[1]] = ws
        a[S:, ws.shape[1]:] = wv
        b = np.zeros((J, D - P, J, a.shape[1]), f32)
        for j in range(J):
            b[j, :, j] = a[P:]
        return a[:P], b.reshape(P, -1)

    def padded(a, n, value=0):
        a = np.asarray(a)
        b = np.full((n,) + a.shape[1:], value, a.dtype)
        b[:a.shape[0]] = a
        return b

    def by_tile(a):
        return np.ascontiguousarray(a.reshape(2 * PAIRS, TILE, -1).transpose(1, 0, 2).reshape(TILE, -1))

    src_p, dst_p = (padded(a, EDGES, N_NODES).astype(np.int32) for a in (src, dst))
    out_v = np.asarray(L0_gnn_W_out_v)
    w2_v = np.asarray(L1_gnn_W2_v)
    a0, b0 = beside(L0_gnn_W_skip0, L0_gnn_W_skip1)
    a1, b1 = beside(L1_gnn_W_sc_s, L1_gnn_W_sc_v)
    arrays = {
        "x_rows": np.concatenate([padded(x, NODES), padded(node_vec1, NODES)], axis=1),
        "src_cols": by_tile(src_p), "dst_cols": by_tile(dst_p),
        "src_rows": src_p.reshape(PAIRS, 2 * TILE), "dst_rows": dst_p.reshape(PAIRS, 2 * TILE),
        "edge_vec": by_tile(padded(edge_attr_3, EDGES, 1)),
        "edge_y": by_tile(padded(edge_attr_4, EDGES)),
        "hidden_in_0": padded(edge_attr_64, EDGES).T, "hidden_in_1": padded(edge_attr_8, EDGES).T,
        "fc1_0": L0_gnn_W_fc1, "fc2_0": L0_gnn_W_fc2, "in_s_0": L0_gnn_W_nl0, "in_v_0": spread(L0_gnn_W_nl1, 5),
        "out_s_0": L0_gnn_W_out_s, "out_a_0": out_v[0:64], "out_b_0": spread(out_v[64:96]), "out_c_0": spread(out_v[96:128]),
        "fc1_1": L1_gnn_fcW1, "fc2_1": L1_gnn_fcW2, "in_s_1": L1_gnn_W1_s, "in_v_1": spread(L1_gnn_W1_v),
        "out_s_1": L1_gnn_W2_s, "out_angle_1": L1_gnn_W3, "out_a_1": w2_v[0:64], "out_b_1": spread(w2_v[64:96]),
        "skip_a_0": a0, "skip_b_0": b0, "skip_a_1": a1, "skip_b_1": b1,
    }
    nc = bacc.Bacc("TRN2", target_bir_lowering=False, num_devices=1)
    feeds, t_in = {}, {}
    for name, a in arrays.items():
        a = np.ascontiguousarray(np.asarray(a))
        feeds["in_" + name] = a
        t_in[name] = nc.dram_tensor("in_" + name, list(a.shape), mb.dt.from_np(a.dtype), kind="ExternalInput").ap()
    out = nc.dram_tensor("out_rows", [NODES, D], mb.dt.float32, kind="ExternalOutput").ap()
    build_gnn(nc, t_in, out)
    r = run_bass_kernel_spmd(nc, [feeds], core_ids=[0])
    return r.results[0]["out_rows"][:N_NODES]
```

```python
import concourse.bass as bass
from concourse import mybir
from contextlib import ExitStack

P = 128
N_NODES, N_EDGES = 100000, 25000
S, V = 64, 32
V3 = 3 * V
D = S + V3
ROW = D + 1
TILE = P
PAIRS = -(-N_EDGES // (2 * TILE))
EDGES = PAIRS * 2 * TILE
J = 4
GROUPS = -(-N_NODES // (P * J))
NODES = GROUPS * P * J
TABLE = NODES + 2 * TILE
OUT0 = 96 + V3
OUT1 = D + 1
EPS = 1e-5


def chunks(words, least, most_words):
    return next(n for n in range(least, words + 1) if words % n == 0 and words // n <= most_words)


ZERO_W = 5600
EDGE_ROUNDS = (PAIRS - 4) // 2 - 2
ZERO_DMAS = (chunks(TABLE * OUT0 // P, 1, ZERO_W), chunks(TABLE * OUT1 // P, EDGE_ROUNDS, ZERO_W))


class Layer:

    def __init__(self, k):
        self.k = k


class Turn:

    def __init__(self, i, offset, unroll, total):
        self.i, self.offset, self.unroll, self.total = i, offset, unroll, total

    def plus(self, d):
        return Turn(self.i, self.offset + d, self.unroll, self.total)

    @property
    def n(self):
        return self.unroll * self.i + self.offset

    def slot(self, ring):
        return self.offset % ring

    @property
    def round(self):
        return self.i + self.offset // self.unroll

    @property
    def half_round(self):
        return 2 * self.i + self.offset // (self.unroll // 2)

    @property
    def halved(self):
        return Turn(self.i, self.offset // 2, self.unroll // 2, self.total // 2)

    @property
    def exists(self):
        return not isinstance(self.i, int) or 0 <= self.n < self.total

    def back(self, d):
        return not isinstance(self.i, int) or self.n >= d


def wait_apart(engine, sem, value):
    engine.wait_ge(sem, value)
    if not isinstance(value, int):
        engine.nop(nofuse=True)


def run_turns(engine, total, unroll, lead, tail, body):
    first = unroll * -(-4 // unroll)
    last = (total - lead) // unroll * unroll
    for s in range(-lead, first):
        body(Turn(0, s, unroll, total))
    with engine.Fori(first // unroll, last // unroll) as i:
        for s in range(unroll):
            body(Turn(i, s, unroll, total))
    for s in range(last, total + tail):
        body(Turn(0, s, unroll, total))


def build_gnn(nc, t_in, out):
    fp32 = mybir.dt.float32
    i32 = mybir.dt.int32
    ALU = mybir.AluOpType
    ACT = mybir.ActivationFunctionType
    AX = mybir.AxisListType

    sums0 = nc.dram_tensor("sums0", [TABLE, OUT0], fp32).ap()
    sums1 = nc.dram_tensor("sums1", [TABLE, OUT1], fp32).ap()
    x1_rows = nc.dram_tensor("x1_rows", [NODES, ROW], fp32).ap()
    unit_rows = nc.dram_tensor("unit_rows", [P, PAIRS * 10], fp32).ap()

    ctx = ExitStack()
    with ctx:
        def sb(name, shape, dt=fp32):
            return ctx.enter_context(nc.sbuf_tensor(name, shape, dt))

        def pb(name, shape, dt=fp32):
            return ctx.enter_context(nc.psum_tensor(name, shape, dt))

        def sem(name):
            return ctx.enter_context(nc.semaphore(name))

        def ring(name, n):
            return [sem(f"{name}_{k}") for k in range(n)]

        ident = sb("ident", [P, P])
        earlier = sb("earlier", [P, 2, 2 * TILE])
        spare_i = sb("spare_i", [P, 2], i32)
        spare = sb("spare", [P, 2])
        minus_half = sb("minus_half", [P, 2 * PAIRS])
        vec = sb("vec", [P, 2 * PAIRS, 3])
        vec_sq = sb("vec_sq", [P, 2 * PAIRS, 3])
        vec_n = sb("vec_n", [P, 2 * PAIRS])
        vec_r = sb("vec_r", [P, 2 * PAIRS])
        unit = sb("unit", [P, 2 * PAIRS, 5])
        zeros = sb("zeros", [P, ZERO_W])
        wt = {n: sb("w_" + n, list(t_in[n].shape)) for n in (
            "fc1_0", "fc2_0", "in_s_0", "in_v_0", "out_s_0", "out_a_0", "out_b_0", "out_c_0",
            "fc1_1", "fc2_1", "in_s_1", "in_v_1", "out_s_1", "out_angle_1", "out_a_1", "out_b_1",
            "skip_s_0", "skip_v_0", "skip_s_1", "skip_v_1")}
        R10, R96 = 10.0 ** -0.5, 96.0 ** -0.5
        weight_scale = {
            "out_s_0": 1 / 32, "out_a_0": 3 ** 0.5 / 32, "out_b_0": 1 / 32, "out_c_0": 1.5 ** 0.5 / 32,
            "fc2_1": 1 / 8, "in_s_1": 1 / 8, "in_v_1": 32 ** -0.5,
            "out_s_1": R10 * R96, "out_angle_1": 0.1 * R10 * R96, "out_a_1": R10 * R96, "out_b_1": R10 * R96,
            "skip_s_1": 1 / 8, "skip_v_1": 32 ** -0.5}

        s_setup = sem("constants_loaded")
        s_zero_tile = sem("zero_tile_ready")
        s_zeroed0, s_zeroed1 = sem("sums0_zeroed"), sem("sums1_zeroed")
        s_pool_const = sem("pool_constants")
        s_spare = sem("spare_ready")
        s_outer_zero = sem("outer_zeroed")
        s_scaled = sem("weights_scaled")
        s_vec_sq, s_vec_n, s_vec_r, s_unit = sem("vec_squared"), sem("vec_norm"), sem("vec_inverse"), sem("unit_ready")
        s_unit_stored = sem("unit_stored")

        def edge_layer(k):
            L = Layer(k)
            L.hid_in = S if k == 0 else 8
            L.w = 224 if k == 0 else 192
            L.xv = 160 if k == 0 else V3
            L.x = S + L.xv
            L.pw = 352 if k == 0 else 256
            L.blocks = [(0, 96), (96, 64), (160, 96)] + ([(256, 96)] if k == 0 else [])
            L.out = OUT0 if k == 0 else OUT1
            L.s_out = 96 if k == 0 else S
            L.geo = 5 if k == 0 else 4
            L.hidden_dram = t_in["hidden_in_%d" % k]
            L.geo_dram = unit_rows if k == 0 else t_in["edge_y"]
            L.gather_key = t_in["dst_cols" if k == 0 else "src_cols"]
            L.key_cols = t_in["src_cols" if k == 0 else "dst_cols"]
            L.key_rows = t_in["src_rows" if k == 0 else "dst_rows"]
            L.rows = t_in["x_rows"] if k == 0 else x1_rows
            L.sums = sums0 if k == 0 else sums1
            L.zeroed = s_zeroed0 if k == 0 else s_zeroed1
            L.zero_dmas = ZERO_DMAS[k]
            n = lambda x: "%s_%d" % (x, k)
            L.hid = [sb(n("hid%d" % b), [L.hid_in, 2 * TILE]) for b in range(2)]
            L.gidx = [sb(n("gidx%d" % b), [P, 2], i32) for b in range(2)]
            L.kcol = [sb(n("kcol%d" % b), [P, 2], i32) for b in range(2)]
            L.krow = [sb(n("krow%d" % b), [P, 2 * TILE], i32) for b in range(2)]
            L.geom = [sb(n("geom%d" % b), [P, 2, L.geo]) for b in range(2)]
            L.geo_s = [sb(n("geos%d" % b), [P, 2, 4]) for b in range(2)]
            L.attr = sb(n("attr"), [P, 2])
            L.got = [sb(n("got%d" % b), [P, 2, ROW]) for b in range(2)]
            L.hT = sb(n("hT"), [S, 2 * TILE])
            L.xsT = sb(n("xsT"), [S, 2, TILE])
            L.xvT = sb(n("xvT"), [V3, 2, TILE])
            L.xs = sb(n("xs"), [P, 2, L.x])
            L.prod = sb(n("prod"), [P, 2, L.pw])
            L.t0, L.t1, L.t2 = (sb(n("t%d" % j), [P, 2, V3]) for j in range(3))
            L.dot = sb(n("dot"), [P, 2, V])
            L.cross = sb(n("cross"), [P, 2, V3])
            L.pT = sb(n("pT"), [96, 2, len(L.blocks), TILE])
            L.msg = sb(n("msg"), [P, 2, L.out])
            L.outer = sb(n("outer"), [P, 2, L.out])
            L.same = [sb(n("same%d" % b), [P, 2, 2 * TILE]) for b in range(2)]
            L.key = sb(n("key"), [P, 2])
            L.junk = sb(n("junk"), [P, 2, 2 * TILE])
            L.before = sb(n("before"), [P, 2])
            L.away = sb(n("away"), [P, 2])
            L.move = sb(n("move"), [P, 2])
            L.sidx = [sb(n("sidx%d" % b), [P, 2], i32) for b in range(2)]
            L.acc = [sb(n("acc%d" % b), [P, 2, L.out]) for b in range(2)]
            L.hidden_loaded = ring(n("hidden_loaded"), 2)
            L.gidx_loaded = ring(n("gidx_loaded"), 2)
            L.keys_loaded = ring(n("keys_loaded"), 2)
            L.geom_loaded = ring(n("geom_loaded"), 2)
            L.gathered = ring(n("gathered"), 2)
            L.scattered = ring(n("scattered"), 2)
            L.features_up = sem(n("features_up"))
            L.lhs_ready = sem(n("lhs_ready"))
            L.wx_done = sem(n("wx_done"))
            L.x_ready = sem(n("x_ready"))
            L.products_ready = sem(n("products_ready"))
            L.pt_done = sem(n("pt_done"))
            L.pt_ready = sem(n("pt_ready"))
            L.m_done = sem(n("m_done"))
            L.msg_ready = sem(n("msg_ready"))
            L.same_ready = sem(n("same_ready"))
            L.sidx_ready = sem(n("sidx_ready"))
            L.c_done = sem(n("c_done"))
            L.acc_ready = sem(n("acc_ready"))
            L.key_ready = sem(n("key_ready"))
            L.before_ready = sem(n("before_ready"))
            L.away_ready = sem(n("away_ready"))
            L.move_ready = sem(n("move_ready"))
            L.t0_ready = sem(n("t0_ready"))
            L.cross_parts = sem(n("cross_parts"))
            L.dot_ready = sem(n("dot_ready"))
            L.cross_ready = sem(n("cross_ready"))
            L.outer_ready = sem(n("outer_ready"))
            L.geo_ready = sem(n("geo_ready"))
            return L

        layers = [edge_layer(0), edge_layer(1)]

        bank = [pb("bank%d" % k, [P, 512]) for k in range(4)]
        wide = [pb("wide%d" % k, [P, 1024]) for k in range(2)]
        pH = bank[0][:, 0:2 * TILE]
        pXT = bank[1]
        pC = bank[2]
        pM = bank[3]
        pPT = wide[0]
        pW = wide[1][:, 0:512]
        pX = wide[1][:, 512:1024]

        RING, HALF_RING = 6, 3
        node_x = [sb("node_x%d" % b, [P, J, ROW]) for b in range(RING)]
        node_sums = [sb("node_sums%d" % b, [P, J, OUT0]) for b in range(RING)]
        node_xsT = [sb("node_xsT%d" % b, [S, J, P]) for b in range(2)]
        node_xvT = [sb("node_xvT%d" % b, [V3, J, P]) for b in range(2)]
        node_t = [sb("node_t%d" % b, [P, J, OUT0]) for b in range(2)]
        node_y = [sb("node_y%d" % b, [P, J, D]) for b in range(HALF_RING)]
        node_res = [sb("node_res%d" % b, [P, J, ROW]) for b in range(HALF_RING)]
        node_gate = [sb("node_gate%d" % b, [P, J, V]) for b in range(2)]
        node_stats = sb("node_stats", [P, J, 6])
        node_mv = [sb("node_mv%d" % b, [P, J, 2]) for b in range(2)]
        node_varp = sb("node_varp", [P, J])
        node_meanr = sb("node_meanr", [P, J])
        node_rstd = [sb("node_rstd%d" % b, [P, J]) for b in range(2)]
        node_shift = [sb("node_shift%d" % b, [P, J]) for b in range(2)]
        angle, turns, part, rest = (sb("angle_%s" % n, [P, 2, J]) for n in ("raw", "turns", "part", "rest"))
        reduced = sb("angle_reduced", [P, 2 * J])
        sine, half_sine = sb("sine", [P, 2, J]), sb("half_sine", [P, 2, J])
        square, cosine = sb("square", [P, 2, J]), sb("cosine", [P, 2, J])
        by_cos = [sb("by_cos%d" % b, [P, 2, J]) for b in range(3)]
        by_sin = [sb("by_sin%d" % b, [P, 2, J]) for b in range(3)]

        def node_layer(k):
            L = Layer(k)
            L.sums_w = OUT0 if k == 0 else OUT1
            L.x_dram = t_in["x_rows"] if k == 0 else x1_rows
            L.sums = sums0 if k == 0 else sums1
            L.out_w = ROW if k == 0 else D
            L.out_dram = x1_rows if k == 0 else out
            n = lambda x: "%s_n%d" % (x, k)

            def packed(t, w):
                return t[:, :, :].rearrange("p j w -> p (j w)")[:, 0:J * w]

            L.x = [t[:, :, :] for t in node_x]
            L.agg_flat = [packed(t, L.sums_w) for t in node_sums]
            L.agg = [t.rearrange("p (j w) -> p j w", w=L.sums_w) for t in L.agg_flat]
            L.res_flat = [packed(t, L.out_w) for t in node_res]
            L.res = [t.rearrange("p (j w) -> p j w", w=L.out_w) for t in L.res_flat]
            L.x_loaded, L.sums_loaded = ring(n("x_loaded"), RING), ring(n("sums_loaded"), RING)
            L.stored = ring(n("stored"), HALF_RING)
            L.xt_done, L.xt_ready, L.o_done = sem(n("xt_done")), sem(n("xt_ready")), sem(n("o_done"))
            L.y_ready, L.stats_ready, L.mv_ready = sem(n("y_ready")), sem(n("stats_ready")), sem(n("mv_ready"))
            L.varp_ready, L.rstd_ready = sem(n("varp_ready")), sem(n("rstd_ready"))
            L.meanr_ready, L.shift_ready, L.norm_ready = sem(n("meanr_ready")), sem(n("shift_ready")), sem(n("norm_ready"))
            if k == 0:
                L.t_ready, L.silu_ready, L.tanh_ready = sem(n("t_ready")), sem(n("silu_ready")), sem(n("tanh_ready"))
                L.gate_ready, L.gated_ready, L.attr_copied = sem(n("gate_ready")), sem(n("gated_ready")), sem(n("attr_copied"))
            else:
                L.angle_step, L.angle_ready, L.sin_ready = sem(n("angle_step")), sem(n("angle_ready")), sem(n("sin_ready"))
                L.factor_step, L.factors_ready, L.z1_ready = sem(n("factor_step")), sem(n("factors_ready")), sem(n("z1_ready"))
            return L

        nodes = [node_layer(0), node_layer(1)]

        def group(dram, turn, w):
            return dram[0:NODES, :].rearrange("(g p j) w -> g p (j w)", p=P, j=J)[turn.n]

        block = ctx.enter_context(nc.Block())

        def zero_part(sp, k, i):
            w = TABLE * (OUT0, OUT1)[k] // P // ZERO_DMAS[k]
            parts = (sums0, sums1)[k].rearrange("r w -> (r w)").rearrange("(n p w) -> n p w", p=P, w=w)
            sp.dma_start(parts[i], zeros[:, 0:w]).then_inc((s_zeroed0, s_zeroed1)[k], 16)

        def sync_edges(sp, L):
            if L.k == 0:
                sp.wait_ge(s_unit_stored, 16)
                for i in range(EDGE_ROUNDS, ZERO_DMAS[1]):
                    zero_part(sp, 1, i)

            def turn(s):
                if L.k == 0 and not isinstance(s.i, int) and s.offset == 0:
                    zero_part(sp, 1, s.i - 2)
                t = s.plus(4)
                if t.exists:
                    b = t.slot(2)
                    if t.back(2):
                        sp.wait_ge(L.gathered[b], 32 * t.round)
                    sp.dma_start(L.gidx[b][:, :], L.gather_key[:, bass.ds(2 * t.n, 2)]).then_inc(L.gidx_loaded[b], 16)
                t = s.plus(3)
                if t.exists:
                    b = t.slot(2)
                    if t.back(2):
                        sp.wait_ge(L.features_up, t.n - 1)
                    sp.dma_start(L.hid[b][:, :], L.hidden_dram[:, bass.ds(2 * TILE * t.n, 2 * TILE)]).then_inc(L.hidden_loaded[b], 16)
                t = s.plus(2)
                if t.exists:
                    b = t.slot(2)
                    if t.back(2):
                        sp.wait_ge(L.same_ready, t.n - 1)
                    sp.dma_start(L.kcol[b][:, :], L.key_cols[:, bass.ds(2 * t.n, 2)]).then_inc(L.keys_loaded[b], 16)
                    sp.dma_start(L.krow[b][:, :], L.key_rows[bass.ds(t.n, 1), :].to_broadcast((P, 2 * TILE))).then_inc(L.keys_loaded[b], 16)
                    if t.back(2):
                        sp.wait_ge(L.msg_ready, t.n - 1)
                    sp.dma_start(L.geom[b][:, :, :].rearrange("p a g -> p (a g)"),
                                 L.geo_dram[:, bass.ds(2 * L.geo * t.n, 2 * L.geo)]).then_inc(L.geom_loaded[b], 16)

            run_turns(sp, PAIRS, 2, 4, 1, turn)

        def sync_nodes(sp, L):
            def turn(s):
                t = s.plus(4)
                if t.exists:
                    b = t.slot(RING)
                    if t.back(RING):
                        sp.wait_ge(L.y_ready, t.n - RING + 1)
                        if L.k == 0:
                            sp.wait_ge(L.t_ready, t.n - RING + 1)
                            sp.wait_ge(L.attr_copied, t.n - RING + 1)
                    sp.dma_start(node_x[b][:, :, :].rearrange("p j w -> p (j w)"), group(L.x_dram, t, ROW)).then_inc(L.x_loaded[b], 16)
                    sp.dma_start(L.agg_flat[b], group(L.sums, t, L.sums_w)).then_inc(L.sums_loaded[b], 16)
                t = s.plus(-3 + L.k)
                if t.exists:
                    b = t.slot(HALF_RING)
                    sp.wait_ge(L.norm_ready, t.n + 1)
                    if L.k == 0:
                        sp.wait_ge(L.attr_copied, t.n + 1)
                    sp.dma_start(group(L.out_dram, t, L.out_w), L.res_flat[b]).then_inc(L.stored[b], 16)

            run_turns(sp, GROUPS, RING, 4, 3, turn)

        def wait_stored(engine, L):
            for b in range(HALF_RING):
                engine.wait_ge(L.stored[b], 16 * len(range(b, GROUPS, HALF_RING)))

        @block.sync
        def _(sp):
            sp.dma_start(vec[:, :, :].rearrange("p t c -> p (t c)"), t_in["edge_vec"]).then_inc(s_setup, 16)
            for n in wt:
                sp.dma_start(wt[n][:, :], t_in[n]).then_inc(s_setup, 16)
            sp.wait_ge(s_zero_tile, 1)
            with sp.Fori(0, ZERO_DMAS[0]) as i:
                zero_part(sp, 0, i)
            sp.wait_ge(s_unit, 1)
            sp.dma_start(unit_rows, unit[:, :, :].rearrange("p t c -> p (t c)")).then_inc(s_unit_stored, 16)
            sync_edges(sp, layers[0])
            for b in range(2):
                sp.wait_ge(layers[0].scattered[b], 32 * (PAIRS // 2))
            sync_nodes(sp, nodes[0])
            wait_stored(sp, nodes[0])
            sync_edges(sp, layers[1])
            for b in range(2):
                sp.wait_ge(layers[1].scattered[b], 32 * (PAIRS // 2))
            sync_nodes(sp, nodes[1])
            wait_stored(sp, nodes[1])

        def pool_edges(pool, L):
            def turn(s):
                t = s.plus(3)
                if t.exists:
                    b = t.slot(2)
                    if t.back(2):
                        pool.wait_ge(L.features_up, t.n - 1)
                        if L.k == 1:
                            pool.wait_ge(L.lhs_ready, t.n - 1)
                    wait_apart(pool, L.gidx_loaded[b], 16 * (t.round + 1))
                    for a in range(2):
                        nc.gpsimd.indirect_dma_start(
                            L.got[b][:, a, :], None, L.rows, bass.IndirectOffsetOnAxis(ap=L.gidx[b][:, a:a + 1], axis=0)
                        ).then_inc(L.gathered[b], 16)
                t = s.plus(-1)
                if t.exists:
                    b = t.slot(2)
                    pool.wait_ge(L.acc_ready, t.n + 1)
                    pool.wait_ge(L.sidx_ready, t.n + 1)
                    if t.back(1):
                        u = t.plus(-1)
                        wait_apart(pool, L.scattered[u.slot(2)], 32 * (u.round + 1))
                    else:
                        pool.wait_ge(L.zeroed, 16 * L.zero_dmas)
                    for a in range(2):
                        nc.gpsimd.indirect_dma_start(
                            L.sums, bass.IndirectOffsetOnAxis(ap=L.sidx[b][:, a:a + 1], axis=0), L.acc[b][:, a, :], None,
                            bounds_check=TABLE - 1, oob_is_err=True, compute_op=ALU.add,
                        ).then_inc(L.scattered[b], 16)

            run_turns(pool, PAIRS, 2, 4, 1, turn)

        def pool_norm(pool, L, t):
            b = t.slot(2)
            gp = nc.gpsimd
            wait_apart(pool, L.mv_ready, t.n + 1)
            gp.tensor_scalar(node_varp[:, :], node_mv[b][:, :, 1], EPS, None, ALU.add).then_inc(L.varp_ready, 1)
            pool.wait_ge(L.varp_ready, t.n + 1)
            if t.back(2):
                pool.wait_ge(L.norm_ready, t.n - 1)
            gp.tensor_tensor(node_rstd[b][:, :], node_varp[:, :], minus_half[:, 0:J], ALU.pow).then_inc(L.rstd_ready, 1)
            pool.wait_ge(L.rstd_ready, t.n + 1)
            gp.tensor_tensor(node_meanr[:, :], node_mv[b][:, :, 0], node_rstd[b][:, :], ALU.mult).then_inc(L.meanr_ready, 1)
            wait_apart(pool, L.meanr_ready, t.n + 1)
            gp.tensor_scalar(node_shift[b][:, :], node_meanr[:, :], -1.0, None, ALU.mult).then_inc(L.shift_ready, 1)

        def pool_nodes0(pool, L):
            gp = nc.gpsimd

            def turn(s):
                t = s.plus(-2)
                if t.exists:
                    pool_norm(pool, L, t)
                t = s
                if t.exists:
                    b, b6 = t.slot(HALF_RING), t.slot(RING)
                    if t.back(HALF_RING):
                        pool.wait_ge(L.stored[b], 16 * t.half_round)
                    wait_apart(pool, L.x_loaded[b6], 16 * (t.round + 1))
                    gp.tensor_copy(L.res[b][:, :, D:ROW], L.x[b6][:, :, D:ROW]).then_inc(L.attr_copied, 1)
                    pool.wait_ge(L.silu_ready, t.n + 1)
                    pool.wait_ge(L.gated_ready, t.n + 1)
                    gp.tensor_tensor(node_y[b][:, :, :], node_y[b][:, :, :], L.x[b6][:, :, 0:D], ALU.add).then_inc(L.y_ready, 1)

            run_turns(pool, GROUPS, RING, 4, 3, turn)

        TWO_PI = [6.28125, 0.0019350051879882812, 3.0199159819567e-07]
        ROUNDER = 12582912.0
        ANGLE_STEPS, FACTOR_STEPS = 10, 2

        def pool_nodes1(pool, L):
            gp = nc.gpsimd

            def angles(t, h):
                done = [0]

                def step(ins):
                    done[0] += 1
                    ins.then_inc(L.angle_step, 1)
                    wait_apart(pool, L.angle_step, ANGLE_STEPS * h.n + done[0])

                for g in range(2):
                    b6 = t.plus(g).slot(RING)
                    pool.wait_ge(L.x_loaded[b6], 16 * (t.plus(g).round + 1))
                    pool.wait_ge(L.sums_loaded[b6], 16 * (t.plus(g).round + 1))
                    step(gp.tensor_tensor(angle[:, g, :], L.agg[b6][:, :, D], L.x[b6][:, :, D], ALU.mult))
                step(gp.tensor_scalar(turns[:, :, :], angle[:, :, :], 0.15915494309189535, ROUNDER, ALU.mult, ALU.add))
                step(gp.tensor_scalar(turns[:, :, :], turns[:, :, :], ROUNDER, None, ALU.subtract))
                left = angle
                for c in TWO_PI:
                    step(gp.tensor_scalar(part[:, :, :], turns[:, :, :], c, None, ALU.mult))
                    step(gp.tensor_tensor(rest[:, :, :], left[:, :, :], part[:, :, :], ALU.subtract))
                    left = rest
                if h.back(1):
                    wait_apart(pool, L.sin_ready, h.n)
                gp.tensor_scalar(reduced[:, :], rest[:, :, :].rearrange("p g j -> p (g j)"), 3.1415925, -3.1415925,
                                 ALU.min, ALU.max).then_inc(L.angle_ready, 1)

            def factors(t, h):
                b = h.slot(3)
                done = [0]

                def step(ins):
                    done[0] += 1
                    ins.then_inc(L.factor_step, 1)
                    wait_apart(pool, L.factor_step, FACTOR_STEPS * h.n + done[0])

                pool.wait_ge(L.sin_ready, h.n + 1)
                step(gp.tensor_tensor(square[:, :, :], half_sine[:, :, :], half_sine[:, :, :], ALU.mult))
                step(gp.tensor_scalar(cosine[:, :, :], square[:, :, :], -2.0, 1.0, ALU.mult, ALU.add))
                if h.back(3):
                    pool.wait_ge(L.y_ready, t.n - 4)
                for g in range(2):
                    attr = L.x[t.plus(g).slot(RING)][:, :, D]
                    gp.tensor_tensor(by_sin[b][:, g, :], sine[:, g, :], attr, ALU.mult)
                    last = gp.tensor_tensor(by_cos[b][:, g, :], cosine[:, g, :], attr, ALU.mult)
                last.then_inc(L.factors_ready, 1)

            def turn(s):
                t = s.plus(-1)
                if t.exists:
                    pool_norm(pool, L, t)
                if s.offset % 2 == 0:
                    t = s.plus(2)
                    if t.exists:
                        angles(t, t.halved)
                else:
                    t = s.plus(1)
                    if t.exists:
                        factors(t, t.halved)

            run_turns(pool, GROUPS, RING, 4, 3, turn)

        @block.gpsimd
        def _(pool):
            gp = nc.gpsimd
            gp.memset(zeros[:, :], 0.0).then_inc(s_zero_tile, 1)
            gp.memset(minus_half[:, :], -0.5)
            gp.memset(ident[:, :], 0.0).then_inc(s_pool_const, 1)
            gp.memset(earlier[:, :, :], 1.0).then_inc(s_pool_const, 1)
            pool.wait_ge(s_pool_const, 2)
            gp.affine_select(out=ident[:, :], in_=ident[:, :], compare_op=ALU.not_equal, fill=1.0, base=0,
                             pattern=[[-1, P]], channel_multiplier=1).then_inc(s_pool_const, 1)
            for a in range(2):
                gp.affine_select(out=earlier[:, a, :], in_=earlier[:, a, :], compare_op=ALU.is_gt, fill=0.0, base=TILE * a,
                                 pattern=[[-1, 2 * TILE]], channel_multiplier=1).then_inc(s_pool_const, 1)
            gp.iota(spare_i[:, :], pattern=[[TILE, 2]], base=NODES, channel_multiplier=1).then_inc(s_spare, 1)
            pool.wait_ge(s_spare, 1)
            gp.tensor_copy(spare[:, :], spare_i[:, :]).then_inc(s_pool_const, 1)
            pool.wait_ge(s_pool_const, 6)
            pool.wait_ge(s_vec_n, 1)
            gp.tensor_tensor(vec_r[:, :], vec_n[:, :], minus_half[:, :], ALU.pow).then_inc(s_vec_r, 1)
            pool_edges(pool, layers[0])
            pool_nodes0(pool, nodes[0])
            wait_stored(pool, nodes[0])
            pool_edges(pool, layers[1])
            pool_nodes1(pool, nodes[1])

        def pe_edges(pe, L):
            mm = nc.tensor.matmul
            fc1, fc2 = wt["fc1_%d" % L.k], wt["fc2_%d" % L.k]
            in_s, in_v = wt["in_s_%d" % L.k], wt["in_v_%d" % L.k]
            W = pW[:, 0:2 * L.w].rearrange("p (a w) -> p a w", a=2)
            X = pX[:, 0:2 * L.x].rearrange("p (a w) -> p a w", a=2)
            nb = len(L.blocks)
            PT = pPT[:, 0:2 * 512].rearrange("p (a n e) -> p a n e", a=2, e=TILE)
            M = pM[:, 0:448].rearrange("p (a w) -> p a w", a=2)
            C = pC[:, 0:2 * L.out].rearrange("p (a w) -> p a w", a=2)

            def turn(s):
                t = s.plus(1)
                if t.exists:
                    pe.wait_ge(L.lhs_ready, t.n + 1)
                    if t.back(1):
                        pe.wait_ge(L.products_ready, t.n)
                    for a in range(2):
                        e = bass.ds(a * TILE, TILE)
                        mm(W[:, a, :], L.hT[:, e], fc2[:, :], start=True, stop=True)
                        mm(X[:, a, 0:S], L.xsT[:, a, :], in_s[:, :], start=True, stop=True)
                        last = mm(X[:, a, S:L.x], L.xvT[:, a, :], in_v[:, :], start=True, stop=True)
                    last.then_inc(L.wx_done, 1)
                t = s.plus(-1)
                if t.exists:
                    b = t.slot(2)
                    pe.wait_ge(L.msg_ready, t.n + 1)
                    pe.wait_ge(L.same_ready, t.n + 1)
                    if t.back(1):
                        pe.wait_ge(L.acc_ready, t.n)
                    for j in range(2):
                        for a in range(2):
                            last = mm(C[:, j, :], L.same[b][:, a, j * TILE:(j + 1) * TILE], L.msg[:, a, :],
                                      start=(a == 0), stop=(a == 1))
                    last.then_inc(L.c_done, 1)
                t = s
                if t.exists:
                    pe.wait_ge(L.products_ready, t.n + 1)
                    if t.back(1):
                        pe.wait_ge(L.pt_ready, t.n)
                    for a in range(2):
                        for n, (c, w) in enumerate(L.blocks):
                            last = nc.tensor.transpose(PT[0:w, a, n, :], L.prod[:, a, c:c + w], ident[:, :])
                    last.then_inc(L.pt_done, 1)
                t = s.plus(2)
                if t.exists:
                    b = t.slot(2)
                    if t.back(1):
                        pe.wait_ge(L.lhs_ready, t.n)
                    pe.wait_ge(L.gathered[b], 32 * (t.round + 1))
                    wait_apart(pe, L.hidden_loaded[b], 16 * (t.round + 1))
                    mm(pH[0:S, :], fc1[:, :], L.hid[b][:, :], start=True, stop=True)
                    for a in range(2):
                        nc.tensor.transpose(pXT[0:S, a * TILE:(a + 1) * TILE], L.got[b][:, a, 0:S], ident[:, :])
                        last = nc.tensor.transpose(pXT[0:V3, (2 + a) * TILE:(3 + a) * TILE], L.got[b][:, a, S:D], ident[:, :])
                    last.then_inc(L.features_up, 1)
                t = s
                if t.exists:
                    pe.wait_ge(L.pt_ready, t.n + 1)
                    if t.back(1):
                        pe.wait_ge(L.msg_ready, t.n)
                    so = L.s_out
                    for a in range(2):
                        last = mm(M[:, a, 0:so], L.pT[:, a, 0, :], wt["out_s_%d" % L.k][:, :], start=True, stop=True)
                        if L.k == 0:
                            mm(M[:, a, 96:192], L.pT[:, a, 2, :], wt["out_b_0"][:, :], start=True, stop=False)
                            mm(M[:, a, 96:192], L.pT[:, a, 3, :], wt["out_c_0"][:, :], start=False, stop=True)
                            last = mm(M[:, a, 192:224], L.pT[0:S, a, 1, :], wt["out_a_0"][:, :], start=True, stop=True)
                        else:
                            mm(M[:, a, 160:161], L.pT[:, a, 0, :], wt["out_angle_1"][:, :], start=True, stop=True)
                            mm(M[:, a, 64:160], L.pT[:, a, 2, :], wt["out_b_1"][:, :], start=True, stop=True)
                            last = mm(M[:, a, 192:224], L.pT[0:S, a, 1, :], wt["out_a_1"][:, :], start=True, stop=True)
                    last.then_inc(L.m_done, 1)

            run_turns(pe, PAIRS, 2, 4, 1, turn)

        xt_psum = [wide[0], wide[1]]
        o_psum = [[bank[0], bank[1]], [bank[2], bank[3]]]

        def pe_nodes(pe, L):
            mm = nc.tensor.matmul
            ws, wv = wt["skip_s_%d" % L.k], wt["skip_v_%d" % L.k]
            so = 96 if L.k == 0 else S

            def turn(s):
                t = s.plus(2)
                if t.exists:
                    b, b6 = t.slot(2), t.slot(RING)
                    xt = xt_psum[b]
                    pe.wait_ge(L.x_loaded[b6], 16 * (t.round + 1))
                    if t.back(2):
                        wait_apart(pe, L.xt_ready, t.n - 1)
                    for j in range(J):
                        nc.tensor.transpose(xt[0:S, j * P:(j + 1) * P], L.x[b6][:, j, 0:S], ident[:, :])
                        last = nc.tensor.transpose(xt[0:V3, (J + j) * P:(J + j + 1) * P], L.x[b6][:, j, S:D], ident[:, :])
                    last.then_inc(L.xt_done, 1)
                t = s.plus(1)
                if t.exists:
                    b = t.slot(2)
                    pe.wait_ge(L.xt_ready, t.n + 1)
                    if t.back(2):
                        pe.wait_ge(L.t_ready if L.k == 0 else L.z1_ready, t.n - 1)
                    for j in range(J):
                        o = o_psum[b][j // 2][:, (j % 2) * 256:(j % 2 + 1) * 256]
                        mm(o[:, 0:so], node_xsT[b][:, j, :], ws[:, :], start=True, stop=True)
                        last = mm(o[:, so:so + V3], node_xvT[b][:, j, :], wv[:, :], start=True, stop=True)
                    last.then_inc(L.o_done, 1)

            run_turns(pe, GROUPS, RING, 4, 3, turn)

        @block.tensor
        def _(pe):
            pe.wait_ge(s_pool_const, 6)
            pe.wait_ge(s_scaled, 1)
            pe_edges(pe, layers[0])
            pe_nodes(pe, nodes[0])
            pe_edges(pe, layers[1])
            pe_nodes(pe, nodes[1])

        def act_edges(act, L):
            nb = len(L.blocks)
            X = pX[:, 0:2 * L.x]
            PT = pPT[:, 0:2 * 512].rearrange("p (a n e) -> p a (n e)", a=2, e=TILE)
            M = pM[:, 0:448].rearrange("p (a w) -> p a w", a=2)
            copy, cp = nc.scalar.activation, ACT.Copy

            def turn(s):
                t = s.plus(1)
                if t.exists:
                    act.wait_ge(L.wx_done, t.n + 1)
                    if t.back(1):
                        act.wait_ge(L.products_ready, t.n)
                    copy(L.xs[:, :, :].rearrange("p a w -> p (a w)"), X, cp).then_inc(L.x_ready, 1)
                t = s.plus(-1)
                if t.exists:
                    b = t.slot(2)
                    act.wait_ge(L.c_done, t.n + 1)
                    if t.back(2):
                        act.wait_ge(L.scattered[b], 32 * t.round)
                    copy(L.acc[b][:, :, :].rearrange("p a w -> p (a w)"), pC[:, 0:2 * L.out], cp).then_inc(L.acc_ready, 1)
                t = s
                if t.exists:
                    act.wait_ge(L.pt_done, t.n + 1)
                    if t.back(1):
                        act.wait_ge(L.m_done, t.n)
                    for lo, hi, rows in ((0, 1, 96), (1, 2, S), (2, nb, 96)):
                        last = copy(L.pT[0:rows, :, lo:hi, :].rearrange("p a n e -> p a (n e)"),
                                    PT[0:rows, :, lo * TILE:hi * TILE], cp)
                    last.then_inc(L.pt_ready, 1)
                t = s.plus(2)
                if t.exists:
                    b = t.slot(2)
                    act.wait_ge(L.features_up, t.n + 1)
                    if t.back(1):
                        act.wait_ge(L.wx_done, t.n)
                    if L.k == 0:
                        copy(L.hT[:, :], pH[0:S, :], ACT.Relu)
                    else:
                        copy(L.hT[:, :], pH[0:S, :], ACT.Silu, scale=8.0 ** -0.5)
                        if t.back(1):
                            act.wait_ge(L.geo_ready, t.n)
                        copy(L.attr[:, :], L.got[b][:, :, D], cp)
                    copy(L.xsT[:, :, :].rearrange("p a e -> p (a e)"), pXT[0:S, 0:2 * TILE], cp)
                    copy(L.xvT[:, :, :].rearrange("p a e -> p (a e)"), pXT[0:V3, 2 * TILE:4 * TILE], cp).then_inc(L.lhs_ready, 1)

            run_turns(act, PAIRS, 2, 4, 1, turn)

        def act_nodes(act, L):
            f = nc.scalar.activation

            def turn(s):
                t = s
                if t.exists and L.k == 0:
                    b, b3 = t.slot(2), t.slot(HALF_RING)
                    act.wait_ge(L.t_ready, t.n + 1)
                    if t.back(3):
                        act.wait_ge(L.norm_ready, t.n - 2)
                    f(node_y[b3][:, :, 0:S], node_t[b][:, :, 0:S], ACT.Silu).then_inc(L.silu_ready, 1)
                    if t.back(2):
                        act.wait_ge(L.gated_ready, t.n - 1)
                    f(node_gate[b][:, :, :], node_t[b][:, :, S:96], ACT.Tanh, scale=0.5).then_inc(L.tanh_ready, 1)
                t = s.plus(2)
                if t.exists:
                    b = t.slot(2)
                    act.wait_ge(L.xt_done, t.n + 1)
                    if t.back(2):
                        act.wait_ge(L.o_done, t.n - 1)
                    f(node_xsT[b][:, :, :].rearrange("p n e -> p (n e)"), xt_psum[b][0:S, 0:512], ACT.Copy)
                    f(node_xvT[b][:, :, :].rearrange("p n e -> p (n e)"), xt_psum[b][0:V3, 512:1024], ACT.Copy).then_inc(L.xt_ready, 1)
                t = s.plus(-2 + L.k)
                if t.exists:
                    b, b3 = t.slot(2), t.slot(HALF_RING)
                    act.wait_ge(L.shift_ready, t.n + 1)
                    if t.back(HALF_RING):
                        act.wait_ge(L.stored[b3], 16 * t.half_round)
                    for j in range(J):
                        last = f(L.res[b3][:, j, 0:D], node_y[b3][:, j, :], ACT.Identity,
                                 bias=node_shift[b][:, j:j + 1], scale=node_rstd[b][:, j:j + 1])
                    last.then_inc(L.norm_ready, 1)
                t = s.plus(2)
                if L.k == 1 and s.offset % 2 == 0 and t.exists:
                    h = t.halved
                    act.wait_ge(L.angle_ready, h.n + 1)
                    if h.back(1):
                        act.wait_ge(L.factors_ready, h.n)
                    f(sine[:, :, :].rearrange("p g j -> p (g j)"), reduced[:, :], ACT.Sin)
                    f(half_sine[:, :, :].rearrange("p g j -> p (g j)"), reduced[:, :], ACT.Sin, scale=0.5).then_inc(L.sin_ready, 1)

            run_turns(act, GROUPS, RING, 4, 3, turn)

        @block.scalar
        def _(act):
            act.wait_ge(s_setup, 16 * (1 + len(wt)))
            for n, c in weight_scale.items():
                nc.scalar.activation(wt[n][:, :], wt[n][:, :], ACT.Copy, scale=float(c))
            act.drain()
            last = nc.scalar.activation(wt["fc2_1"][:, 160:192], wt["fc2_1"][:, 160:192], ACT.Copy, scale=3 ** -0.5)
            last.then_inc(s_scaled, 1)
            act_edges(act, layers[0])
            act_nodes(act, nodes[0])
            act_edges(act, layers[1])
            act_nodes(act, nodes[1])

        def dve_edges(dve, L):
            v = nc.vector
            W = pW[:, 0:2 * L.w].rearrange("p (a w) -> p a w", a=2)
            M = pM[:, 0:448].rearrange("p (a w) -> p a w", a=2)
            vo = 96 if L.k == 0 else S

            def vec3(x):
                return x.rearrange("p a (m c) -> p a m c", c=3)

            def over3(x):
                return x.unsqueeze(3).to_broadcast((P, 2, V, 3))

            def geo(g, c):
                return g[:, :, c:c + 3].unsqueeze(2).to_broadcast((P, 2, V, 3))

            def turn(s):
                t = s
                if t.exists:
                    b = t.slot(2)
                    dve.wait_ge(L.keys_loaded[b], 32 * (t.round + 1))
                    v.tensor_copy(L.key[:, :], L.kcol[b][:, :]).then_inc(L.key_ready, 1)
                    dve.wait_ge(L.key_ready, t.n + 1)
                    for a in range(2):
                        last = v.scalar_tensor_tensor(L.junk[:, a, :], L.krow[b][:, :], L.key[:, a:a + 1], earlier[:, a, :],
                                                      ALU.is_equal, ALU.mult, accum_out=L.before[:, a:a + 1])
                    last.then_inc(L.before_ready, 1)
                    v.tensor_tensor(L.away[:, :], spare[:, :], L.key[:, :], ALU.subtract).then_inc(L.away_ready, 1)
                    if t.back(2):
                        dve.wait_ge(L.c_done, t.n - 1)
                    for a in range(2):
                        last = v.tensor_scalar(L.same[b][:, a, :], L.krow[b][:, :], L.key[:, a:a + 1], None, ALU.is_equal)
                        if a == 0:
                            dve.wait_ge(L.before_ready, t.n + 1)
                            dve.wait_ge(L.away_ready, t.n + 1)
                            v.scalar_tensor_tensor(L.move[:, :], L.before[:, :], 1.0, L.away[:, :], ALU.min, ALU.mult).then_inc(L.move_ready, 1)
                    last.then_inc(L.same_ready, 1)
                    dve.wait_ge(L.move_ready, t.n + 1)
                    if t.back(2):
                        dve.wait_ge(L.scattered[b], 32 * t.round)
                    v.tensor_tensor(L.sidx[b][:, :], L.move[:, :], L.key[:, :], ALU.add).then_inc(L.sidx_ready, 1)
                t = s.plus(1)
                if t.exists:
                    b = t.slot(2)
                    dve.wait_ge(L.geom_loaded[b], 16 * (t.round + 1))
                    if L.k == 1:
                        dve.wait_ge(L.lhs_ready, t.n + 1)
                        v.tensor_tensor(L.geo_s[b][:, :, :], L.geom[b][:, :, :],
                                        L.attr[:, :].unsqueeze(2).to_broadcast((P, 2, 4)), ALU.mult).then_inc(L.geo_ready, 1)
                        dve.wait_ge(L.geo_ready, t.n + 1)
                    dve.wait_ge(L.x_ready, t.n + 1)
                    if t.back(1):
                        dve.wait_ge(L.pt_done, t.n)
                    xs = L.xs[:, :, 0:S]
                    g = L.geom[b] if L.k == 0 else L.geo_s[b]
                    if L.k == 0:
                        xv = L.xs[:, :, S:S + 160].rearrange("p a (m c) -> p a m c", c=5)
                        v.tensor_tensor(vec3(L.t0[:, :, :]), xv[:, :, :, 0:3], geo(g, 0), ALU.mult).then_inc(L.t0_ready, 1)
                        v.tensor_tensor(vec3(L.t1[:, :, :]), xv[:, :, :, 1:4], geo(g, 2), ALU.mult)
                        v.tensor_tensor(vec3(L.t2[:, :, :]), xv[:, :, :, 2:5], geo(g, 1), ALU.mult).then_inc(L.cross_parts, 1)
                        dve.wait_ge(L.t0_ready, t.n + 1)
                        v.tensor_reduce(L.dot[:, :, :], vec3(L.t0[:, :, :]), AX.X, ALU.add).then_inc(L.dot_ready, 1)
                        dve.wait_ge(L.cross_parts, t.n + 1)
                        v.tensor_tensor(L.cross[:, :, :], L.t1[:, :, :], L.t2[:, :, :], ALU.subtract).then_inc(L.cross_ready, 1)
                        ac = L.prod[:, :, 0:192].rearrange("p a (n c) -> p a n c", c=96)[:, :, :, 0:S]
                        v.tensor_tensor(ac, W[:, :, 0:2 * S].rearrange("p a (n c) -> p a n c", c=S),
                                        xs.unsqueeze(2).to_broadcast((P, 2, 2, S)), ALU.mult)
                        v.tensor_tensor(vec3(L.prod[:, :, 160:256]), over3(W[:, :, 128:160]), xv[:, :, :, 0:3], ALU.mult)
                        dve.wait_ge(L.dot_ready, t.n + 1)
                        v.tensor_tensor(L.prod[:, :, S:96], W[:, :, 160:192], L.dot[:, :, :], ALU.mult)
                        dve.wait_ge(L.cross_ready, t.n + 1)
                        v.tensor_tensor(vec3(L.prod[:, :, 256:352]), over3(W[:, :, 192:224]), vec3(L.cross[:, :, :]),
                                        ALU.mult).then_inc(L.products_ready, 1)
                    else:
                        xv = vec3(L.xs[:, :, S:D])
                        v.tensor_tensor(vec3(L.t0[:, :, :]), xv, geo(g, 1), ALU.mult).then_inc(L.t0_ready, 1)
                        for a in range(2):
                            v.scalar_tensor_tensor(L.prod[:, a, 0:S], W[:, a, 0:S], g[:, a, 0:1], xs[:, a, :], ALU.mult, ALU.mult)
                            v.scalar_tensor_tensor(vec3(L.prod[:, :, 160:256])[:, a], W[:, a, 128:160].unsqueeze(2).to_broadcast((P, V, 3)),
                                                   g[:, a, 0:1], xv[:, a], ALU.mult, ALU.mult)
                        dve.wait_ge(L.t0_ready, t.n + 1)
                        v.tensor_reduce(L.dot[:, :, :], vec3(L.t0[:, :, :]), AX.X, ALU.add).then_inc(L.dot_ready, 1)
                        v.tensor_tensor(L.prod[:, :, 96:160], W[:, :, S:2 * S], xs, ALU.mult)
                        dve.wait_ge(L.dot_ready, t.n + 1)
                        v.tensor_tensor(L.prod[:, :, S:96], W[:, :, 160:192], L.dot[:, :, :], ALU.mult).then_inc(L.products_ready, 1)
                t = s
                if t.exists:
                    b = t.slot(2)
                    g, c = (L.geom[b], 0) if L.k == 0 else (L.geo_s[b], 1)
                    dve.wait_ge(L.m_done, t.n + 1)
                    v.tensor_tensor(vec3(L.outer[:, :, vo:vo + V3]), over3(M[:, :, 192:224]), geo(g, c), ALU.mult).then_inc(L.outer_ready, 1)
                    dve.wait_ge(L.outer_ready, t.n + 1)
                    if t.back(1):
                        dve.wait_ge(L.c_done, t.n)
                    v.tensor_tensor(L.msg[:, :, :], M[:, :, 0:L.out], L.outer[:, :, :], ALU.add).then_inc(L.msg_ready, 1)

            run_turns(dve, PAIRS, 2, 4, 1, turn)

        def dve_stats(dve, L, t):
            v = nc.vector
            b, b3 = t.slot(2), t.slot(HALF_RING)
            for j in range(J):
                last = v.bn_stats(node_stats[:, j, :], node_y[b3][:, j, :])
            last.then_inc(L.stats_ready, 1)
            if t.back(2):
                dve.wait_ge(L.meanr_ready, t.n - 1)
            wait_apart(dve, L.stats_ready, t.n + 1)
            for j in range(J):
                last = v.bn_aggr(node_mv[b][:, j, :], node_stats[:, j, :])
            last.then_inc(L.mv_ready, 1)

        def dve_nodes0(dve, L):
            v = nc.vector

            def turn(s):
                t = s.plus(-1)
                if t.exists:
                    dve.wait_ge(L.y_ready, t.n + 1)
                    dve_stats(dve, L, t)
                t = s
                if t.exists:
                    b, b3 = t.slot(2), t.slot(HALF_RING)
                    dve.wait_ge(L.tanh_ready, t.n + 1)
                    v.tensor_scalar(node_gate[b][:, :, :], node_gate[b][:, :, :], 0.5, 0.5, ALU.mult, ALU.add).then_inc(L.gate_ready, 1)
                    dve.wait_ge(L.gate_ready, t.n + 1)
                    v.tensor_tensor(node_y[b3][:, :, S:D].rearrange("p j (m c) -> p j m c", c=3),
                                    node_t[b][:, :, 96:192].rearrange("p j (m c) -> p j m c", c=3),
                                    node_gate[b][:, :, :].unsqueeze(3).to_broadcast((P, J, V, 3)), ALU.mult).then_inc(L.gated_ready, 1)
                t = s.plus(1)
                if t.exists:
                    b, b6 = t.slot(2), t.slot(RING)
                    dve.wait_ge(L.sums_loaded[b6], 16 * (t.round + 1))
                    dve.wait_ge(L.o_done, t.n + 1)
                    if t.back(2):
                        dve.wait_ge(L.tanh_ready, t.n - 1)
                    for h in range(2):
                        o = o_psum[b][h][:, :].rearrange("p (j w) -> p j w", w=256)[:, :, 0:OUT0]
                        last = v.tensor_tensor(node_t[b][:, 2 * h:2 * h + 2, :], o, L.agg[b6][:, 2 * h:2 * h + 2, :], ALU.add)
                    last.then_inc(L.t_ready, 1)

            run_turns(dve, GROUPS, RING, 4, 3, turn)

        def dve_nodes1(dve, L):
            v = nc.vector

            def turn(s):
                t = s
                if t.exists:
                    b, b3, b6 = t.slot(2), t.slot(HALF_RING), t.slot(RING)
                    h = t.halved
                    fc, fs = by_cos[h.slot(3)][:, t.offset % 2, :], by_sin[h.slot(3)][:, t.offset % 2, :]
                    dve.wait_ge(L.o_done, t.n + 1)
                    dve.wait_ge(L.factors_ready, h.n + 1)
                    if t.back(3):
                        dve.wait_ge(L.norm_ready, t.n - 2)
                    for j in range(J):
                        o = o_psum[b][j // 2][:, (j % 2) * 256:(j % 2) * 256 + D]
                        last = v.scalar_tensor_tensor(node_y[b3][:, j, :], o, fc[:, j:j + 1], L.x[b6][:, j, 0:D], ALU.mult, ALU.add)
                    last.then_inc(L.z1_ready, 1)
                    dve.wait_ge(L.z1_ready, t.n + 1)
                    for j in range(J):
                        last = v.scalar_tensor_tensor(node_y[b3][:, j, :], L.agg[b6][:, j, 0:D], fs[:, j:j + 1], node_y[b3][:, j, :],
                                                      ALU.mult, ALU.add)
                    last.then_inc(L.y_ready, 1)
                    dve.wait_ge(L.y_ready, t.n + 1)
                    dve_stats(dve, L, t)

            run_turns(dve, GROUPS, RING, 4, 3, turn)

        @block.vector
        def _(dve):
            v = nc.vector
            dve.wait_ge(s_setup, 16 * (1 + len(wt)))
            v.tensor_tensor(vec_sq[:, :, :], vec[:, :, :], vec[:, :, :], ALU.mult).then_inc(s_vec_sq, 1)
            dve.wait_ge(s_vec_sq, 1)
            v.tensor_reduce(vec_n[:, :], vec_sq[:, :, :], AX.X, ALU.add).then_inc(s_vec_n, 1)
            dve.wait_ge(s_vec_r, 1)
            for lo, n in ((0, 3), (3, 2)):
                last = v.tensor_tensor(unit[:, :, lo:lo + n], vec[:, :, 0:n],
                                       vec_r[:, :].unsqueeze(2).to_broadcast((P, 2 * PAIRS, n)), ALU.mult)
            last.then_inc(s_unit, 1)
            dve.wait_ge(s_pool_const, 6)
            for L in layers:
                last = v.memset(L.outer[:, :, :], 0.0)
            last.then_inc(s_outer_zero, 1)
            dve.wait_ge(s_outer_zero, 1)
            dve_edges(dve, layers[0])
            dve_nodes0(dve, nodes[0])
            dve_edges(dve, layers[1])
            dve_nodes1(dve, nodes[1])


def kernel(x, src, dst, edge_attr_3, edge_attr_4, edge_attr_64, edge_attr_8, node_vec1, L0_gnn_W_skip0, L0_gnn_W_skip1,
           L0_gnn_W_nl0, L0_gnn_W_nl1, L0_gnn_W_fc1, L0_gnn_W_fc2, L0_gnn_W_out_s, L0_gnn_W_out_v, L1_gnn_W_sc_s,
           L1_gnn_W_sc_v, L1_gnn_W1_s, L1_gnn_W1_v, L1_gnn_W2_s, L1_gnn_W2_v, L1_gnn_W3, L1_gnn_fcW1, L1_gnn_fcW2):
    import numpy as np
    import concourse.bacc as bacc
    from concourse import mybir as mb
    from concourse.bass_utils import run_bass_kernel_spmd

    f32 = np.float32

    def spread(w, width=3):
        w = np.asarray(w)
        m, k = w.shape
        a = np.zeros((m, 3, k, width), f32)
        for c in range(width):
            a[:, c % 3, :, c] = w
        return a.reshape(3 * m, width * k)

    def padded(a, n, value=0):
        a = np.asarray(a)
        b = np.full((n,) + a.shape[1:], value, a.dtype)
        b[:a.shape[0]] = a
        return b

    def by_tile(a):
        return np.ascontiguousarray(a.reshape(2 * PAIRS, TILE, -1).transpose(1, 0, 2).reshape(TILE, -1))

    src_p, dst_p = (padded(a, EDGES, N_NODES).astype(np.int32) for a in (src, dst))
    out_v = np.asarray(L0_gnn_W_out_v)
    w2_v = np.asarray(L1_gnn_W2_v)
    arrays = {
        "x_rows": np.concatenate([padded(x, NODES), padded(node_vec1, NODES)], axis=1),
        "src_cols": by_tile(src_p), "dst_cols": by_tile(dst_p),
        "src_rows": src_p.reshape(PAIRS, 2 * TILE), "dst_rows": dst_p.reshape(PAIRS, 2 * TILE),
        "edge_vec": by_tile(padded(edge_attr_3, EDGES, 1)),
        "edge_y": by_tile(padded(edge_attr_4, EDGES)),
        "hidden_in_0": padded(edge_attr_64, EDGES).T, "hidden_in_1": padded(edge_attr_8, EDGES).T,
        "fc1_0": L0_gnn_W_fc1, "fc2_0": L0_gnn_W_fc2, "in_s_0": L0_gnn_W_nl0, "in_v_0": spread(L0_gnn_W_nl1, 5),
        "out_s_0": L0_gnn_W_out_s, "out_a_0": out_v[0:64], "out_b_0": spread(out_v[64:96]), "out_c_0": spread(out_v[96:128]),
        "fc1_1": L1_gnn_fcW1, "fc2_1": L1_gnn_fcW2, "in_s_1": L1_gnn_W1_s, "in_v_1": spread(L1_gnn_W1_v),
        "out_s_1": L1_gnn_W2_s, "out_angle_1": L1_gnn_W3, "out_a_1": w2_v[0:64], "out_b_1": spread(w2_v[64:96]),
        "skip_s_0": L0_gnn_W_skip0, "skip_v_0": spread(L0_gnn_W_skip1),
        "skip_s_1": L1_gnn_W_sc_s, "skip_v_1": spread(L1_gnn_W_sc_v),
    }
    nc = bacc.Bacc("TRN2", target_bir_lowering=False, num_devices=1)
    feeds, t_in = {}, {}
    for name, a in arrays.items():
        a = np.ascontiguousarray(np.asarray(a))
        feeds["in_" + name] = a
        t_in[name] = nc.dram_tensor("in_" + name, list(a.shape), mb.dt.from_np(a.dtype), kind="ExternalInput").ap()
    out = nc.dram_tensor("out_rows", [NODES, D], mb.dt.float32, kind="ExternalOutput").ap()
    build_gnn(nc, t_in, out)
    r = run_bass_kernel_spmd(nc, [feeds], core_ids=[0])
    return r.results[0]["out_rows"][:N_NODES]
```

```python
import concourse.bass as bass
from concourse import mybir
from contextlib import ExitStack

P = 128
N_NODES, N_EDGES = 100000, 25000
S, V = 64, 32
V3 = 3 * V
D = S + V3
ROW = D + 1
TILE = P
PAIRS = -(-N_EDGES // (2 * TILE))
EDGES = PAIRS * 2 * TILE
J = 4
GROUPS = -(-N_NODES // (P * J))
NODES = GROUPS * P * J
TABLE = -(-(NODES + 2 * TILE) // (12 * P)) * 12 * P
OUT0 = 96 + V3
OUT1 = D + 1
EPS = 1e-5
WARM_PRODUCTS = 4


def chunks(words, least, most_words):
    return next(n for n in range(least, words + 1) if words % n == 0 and words // n <= most_words)


ZERO_W = 5600
LOOPED = (PAIRS - 4) // 2 * 2 - 4
ZERO_DMAS = (chunks(TABLE * OUT0 // P, 1, ZERO_W), chunks(TABLE * OUT1 // P, LOOPED, ZERO_W))


class Layer:

    def __init__(self, k):
        self.k = k


class Turn:

    def __init__(self, i, offset, unroll, total):
        self.i, self.offset, self.unroll, self.total = i, offset, unroll, total

    def plus(self, d):
        return Turn(self.i, self.offset + d, self.unroll, self.total)

    @property
    def n(self):
        return self.unroll * self.i + self.offset

    def slot(self, ring):
        return self.offset % ring

    @property
    def round(self):
        return self.i + self.offset // self.unroll

    @property
    def half_round(self):
        return 2 * self.i + self.offset // (self.unroll // 2)

    @property
    def halved(self):
        return Turn(self.i, self.offset // 2, self.unroll // 2, self.total // 2)

    @property
    def exists(self):
        return not isinstance(self.i, int) or 0 <= self.n < self.total

    def back(self, d):
        return not isinstance(self.i, int) or self.n >= d


def wait_apart(engine, sem, value):
    engine.wait_ge(sem, value)
    if not isinstance(value, int):
        engine.nop(nofuse=True)


def run_turns(engine, total, unroll, lead, tail, body):
    first = unroll * -(-4 // unroll)
    last = (total - lead) // unroll * unroll
    for s in range(-lead, first):
        body(Turn(0, s, unroll, total))
    with engine.Fori(first // unroll, last // unroll) as i:
        for s in range(unroll):
            body(Turn(i, s, unroll, total))
    for s in range(last, total + tail):
        body(Turn(0, s, unroll, total))


def build_gnn(nc, t_in, out):
    fp32 = mybir.dt.float32
    i32 = mybir.dt.int32
    ALU = mybir.AluOpType
    ACT = mybir.ActivationFunctionType
    AX = mybir.AxisListType

    sums0 = nc.dram_tensor("sums0", [TABLE, OUT0], fp32).ap()
    sums1 = nc.dram_tensor("sums1", [TABLE, OUT1], fp32).ap()
    x1_rows = nc.dram_tensor("x1_rows", [NODES, ROW], fp32).ap()
    unit_rows = nc.dram_tensor("unit_rows", [P, PAIRS * 10], fp32).ap()

    ctx = ExitStack()
    with ctx:
        def sb(name, shape, dt=fp32):
            return ctx.enter_context(nc.sbuf_tensor(name, shape, dt))

        def pb(name, shape, dt=fp32):
            return ctx.enter_context(nc.psum_tensor(name, shape, dt))

        def sem(name):
            return ctx.enter_context(nc.semaphore(name))

        def ring(name, n):
            return [sem(f"{name}_{k}") for k in range(n)]

        ident = sb("ident", [P, P])
        earlier = sb("earlier", [P, 2, 2 * TILE])
        spare_i = sb("spare_i", [P, 2], i32)
        spare = sb("spare", [P, 2])
        minus_half = sb("minus_half", [P, 2 * PAIRS])
        vec = sb("vec", [P, 2 * PAIRS, 3])
        vec_sq = sb("vec_sq", [P, 2 * PAIRS, 3])
        vec_n = sb("vec_n", [P, 2 * PAIRS])
        vec_r = sb("vec_r", [P, 2 * PAIRS])
        unit = sb("unit", [P, 2 * PAIRS, 5])
        zeros = sb("zeros", [P, ZERO_W])
        wt = {n: sb("w_" + n, list(t_in[n].shape)) for n in (
            "fc1_0", "fc2_in_s_0", "in_v_0", "out_sa_0", "out_dc_0", "out_b_0",
            "fc1_1", "fc2_in_s_1", "in_v_1", "out_sa_1", "out_db_1",
            "skip_s_0", "skip_v_0", "skip_s_1", "skip_v_1")}
        R10, R96 = 10.0 ** -0.5, 96.0 ** -0.5
        OUT = R10 * R96
        weight_scale = [
            ("out_sa_0", 0, V, 3 ** 0.5 / 64), ("out_sa_0", V, 128, 1 / 32),
            ("out_dc_0", 0, 96, 1 / 32), ("out_dc_0", 96, 192, 1.5 ** 0.5 / 64), ("out_b_0", 0, V3, 1 / 64),
            ("skip_v_0", 0, V3, 1 / 2),
            ("fc2_in_s_1", 0, 160, 1 / 8), ("fc2_in_s_1", 160, 192, 1 / 8 * 3 ** -0.5),
            ("fc2_in_s_1", 192, 256, 1 / 8), ("in_v_1", 0, V3, V ** -0.5),
            ("out_sa_1", 0, V, OUT), ("out_sa_1", V, V + 1, 0.1 * OUT), ("out_sa_1", V + 1, 193, OUT),
            ("out_db_1", 0, 1, 0.1 * OUT), ("out_db_1", 1, 161, OUT),
            ("skip_s_1", 0, D, 1 / 8), ("skip_v_1", 0, V3, V ** -0.5)]

        s_setup = sem("constants_loaded")
        s_zero_tile = sem("zero_tile_ready")
        s_zeroed0, s_zeroed1 = sem("sums0_zeroed"), sem("sums1_zeroed")
        s_pool_const = sem("pool_constants")
        s_spare = sem("spare_ready")
        s_zeros = sem("zeros_ready")
        s_scaled = sem("weights_scaled")
        s_vec_sq, s_vec_n, s_vec_r, s_unit = sem("vec_squared"), sem("vec_norm"), sem("vec_inverse"), sem("unit_ready")
        s_unit_stored = sem("unit_stored")

        def edge_layer(k):
            L = Layer(k)
            L.hid_in = S if k == 0 else 8
            L.w = 224 if k == 0 else 192
            L.xv = 160 if k == 0 else V3
            L.x = S + L.xv
            L.pw = 352 if k == 0 else 256
            L.blocks = [(0, 128), (128, 128)] + ([(256, 96)] if k == 0 else [])
            L.out = OUT0 if k == 0 else OUT1
            L.sa_w = 128 if k == 0 else V + OUT1
            L.vo = 96 if k == 0 else 1 + S
            L.geo = 5 if k == 0 else 4
            L.hidden_dram = t_in["hidden_in_%d" % k]
            L.geo_dram = unit_rows if k == 0 else t_in["edge_y"]
            L.gather_key = t_in["dst_cols" if k == 0 else "src_cols"]
            L.key_cols = t_in["src_cols" if k == 0 else "dst_cols"]
            L.key_rows = t_in["src_rows" if k == 0 else "dst_rows"]
            L.rows = t_in["x_rows"] if k == 0 else x1_rows
            L.sums = sums0 if k == 0 else sums1
            L.zeroed = s_zeroed0 if k == 0 else s_zeroed1
            L.zero_dmas = ZERO_DMAS[k]
            n = lambda x: "%s_%d" % (x, k)
            L.hid = [sb(n("hid%d" % b), [L.hid_in, 2 * TILE]) for b in range(2)]
            L.gidx = [sb(n("gidx%d" % b), [P, 2], i32) for b in range(2)]
            L.kcol = [sb(n("kcol%d" % b), [P, 2], i32) for b in range(2)]
            L.krow = [sb(n("krow%d" % b), [P, 2 * TILE], i32) for b in range(2)]
            L.geom = [sb(n("geom%d" % b), [P, 2, L.geo]) for b in range(2)]
            L.geo_s = [sb(n("geos%d" % b), [P, 2, 4]) for b in range(2)]
            L.attr = sb(n("attr"), [P, 2])
            L.got = [sb(n("got%d" % b), [P, 2, S + ROW]) for b in range(2)]
            L.hsT = sb(n("hsT"), [2 * S, 2 * TILE])
            L.xvT = sb(n("xvT"), [V3, 2, TILE])
            L.xs = sb(n("xs"), [P, 2, L.x])
            L.prod = sb(n("prod"), [P, 2, L.pw])
            L.t0, L.t1, L.t2 = (sb(n("t%d" % j), [P, 2, V3]) for j in range(3))
            L.dot = sb(n("dot"), [P, 2, V])
            L.cross = sb(n("cross"), [P, 2, V3])
            L.pT = sb(n("pT"), [P, 2, len(L.blocks), TILE])
            L.msg = sb(n("msg"), [P, 2, L.out])
            L.outer = sb(n("outer"), [P, 2, L.out])
            L.same = [sb(n("same%d" % b), [P, 2, 2 * TILE]) for b in range(2)]
            L.key = sb(n("key"), [P, 2])
            L.junk = sb(n("junk"), [P, 2, 2 * TILE])
            L.before = sb(n("before"), [P, 2])
            L.away = sb(n("away"), [P, 2])
            L.move = sb(n("move"), [P, 2])
            L.sidx = [sb(n("sidx%d" % b), [P, 2], i32) for b in range(2)]
            L.acc = [sb(n("acc%d" % b), [P, 2, L.out]) for b in range(2)]
            L.hidden_loaded = ring(n("hidden_loaded"), 2)
            L.gidx_loaded = ring(n("gidx_loaded"), 2)
            L.keys_loaded = ring(n("keys_loaded"), 2)
            L.geom_loaded = ring(n("geom_loaded"), 2)
            L.gathered = ring(n("gathered"), 2)
            L.scattered = ring(n("scattered"), 2)
            L.features_up = sem(n("features_up"))
            L.lhs_ready = sem(n("lhs_ready"))
            L.wx_done = sem(n("wx_done"))
            L.x_ready = sem(n("x_ready"))
            L.products_ready = sem(n("products_ready"))
            L.pt_done = sem(n("pt_done"))
            L.pt_ready = sem(n("pt_ready"))
            L.m_done = sem(n("m_done"))
            L.msg_ready = sem(n("msg_ready"))
            L.same_ready = sem(n("same_ready"))
            L.sidx_ready = sem(n("sidx_ready"))
            L.c_done = sem(n("c_done"))
            L.acc_ready = sem(n("acc_ready"))
            L.key_ready = sem(n("key_ready"))
            L.before_ready = sem(n("before_ready"))
            L.away_ready = sem(n("away_ready"))
            L.move_ready = sem(n("move_ready"))
            L.t0_ready = sem(n("t0_ready"))
            L.cross_parts = sem(n("cross_parts"))
            L.dot_ready = sem(n("dot_ready"))
            L.cross_ready = sem(n("cross_ready"))
            L.outer_ready = sem(n("outer_ready"))
            L.geo_ready = sem(n("geo_ready"))
            return L

        layers = [edge_layer(0), edge_layer(1)]

        bank = [pb("bank%d" % k, [P, 512]) for k in range(4)]
        wide = [pb("wide%d" % k, [P, 1024]) for k in range(2)]
        pH = bank[0][:, 0:2 * TILE]
        pXT = bank[1]
        pC = bank[2]
        pM = bank[3]
        pPT = wide[0]
        pWX = wide[1][:, :].rearrange("p (a w) -> p a w", a=2)

        RING, HALF_RING = 8, 4
        node_x = sb("node_x", [P, RING, J, ROW])
        node_sums = sb("node_sums", [P, RING, J * OUT0])
        node_xsT = [sb("node_xsT%d" % b, [S, J, P]) for b in range(2)]
        node_xvT = [sb("node_xvT%d" % b, [V3, J, P]) for b in range(2)]
        node_t = [sb("node_t%d" % b, [P, J, OUT0]) for b in range(2)]
        node_y = [sb("node_y%d" % b, [P, J, D]) for b in range(HALF_RING)]
        node_res = [sb("node_res%d" % b, [P, J, ROW]) for b in range(HALF_RING)]
        node_gate = [sb("node_gate%d" % b, [P, J, V]) for b in range(2)]
        node_stats = sb("node_stats", [P, J, 6])
        node_mv = [sb("node_mv%d" % b, [P, J, 2]) for b in range(2)]
        node_varp = [sb("node_varp%d" % b, [P, J]) for b in range(2)]
        node_meanr = sb("node_meanr", [P, J])
        node_rstd = [sb("node_rstd%d" % b, [P, J]) for b in range(2)]
        node_shift = [sb("node_shift%d" % b, [P, J]) for b in range(2)]
        angle, turns, part, rest = (sb("angle_%s" % n, [P, 2, J]) for n in ("raw", "turns", "part", "rest"))
        reduced = sb("angle_reduced", [P, 2 * J])
        sine, half_sine = sb("sine", [P, 2, J]), sb("half_sine", [P, 2, J])
        square, cosine = sb("square", [P, 2, J]), sb("cosine", [P, 2, J])
        by_cos = [sb("by_cos%d" % b, [P, 2, J]) for b in range(HALF_RING)]
        by_sin = [sb("by_sin%d" % b, [P, 2, J]) for b in range(HALF_RING)]

        def node_layer(k):
            L = Layer(k)
            L.sums_w = OUT0 if k == 0 else OUT1
            L.x_dram = t_in["x_rows"] if k == 0 else x1_rows
            L.sums = sums0 if k == 0 else sums1
            L.out_w = ROW if k == 0 else D
            L.out_dram = x1_rows if k == 0 else out
            n = lambda x: "%s_n%d" % (x, k)

            def packed(t, w):
                return t[:, :, :].rearrange("p j w -> p (j w)")[:, 0:J * w]

            L.x = [node_x[:, b, :, :] for b in range(RING)]
            L.agg_flat = [node_sums[:, b, 0:J * L.sums_w] for b in range(RING)]
            L.agg_ring = node_sums[:, :, 0:J * L.sums_w].rearrange("p b (j w) -> p b j w", w=L.sums_w)
            L.agg = [L.agg_ring[:, b] for b in range(RING)]
            L.res_flat = [packed(t, L.out_w) for t in node_res]
            L.res = [t.rearrange("p (j w) -> p j w", w=L.out_w) for t in L.res_flat]
            L.x_loaded, L.sums_loaded = ring(n("x_loaded"), RING), ring(n("sums_loaded"), RING)
            L.stored = ring(n("stored"), HALF_RING)
            L.xt_done, L.xt_ready, L.o_done = sem(n("xt_done")), sem(n("xt_ready")), sem(n("o_done"))
            L.y_ready, L.stats_ready, L.mv_ready = sem(n("y_ready")), sem(n("stats_ready")), sem(n("mv_ready"))
            L.varp_ready, L.rstd_ready = sem(n("varp_ready")), sem(n("rstd_ready"))
            L.shift_ready, L.norm_ready = sem(n("shift_ready")), sem(n("norm_ready"))
            if k == 0:
                L.t_ready, L.silu_ready, L.tanh_ready = sem(n("t_ready")), sem(n("silu_ready")), sem(n("tanh_ready"))
                L.gated_ready, L.attr_copied = sem(n("gated_ready")), sem(n("attr_copied"))
            else:
                L.meanr_ready = sem(n("meanr_ready"))
                L.angle_step, L.angle_ready, L.sin_ready = sem(n("angle_step")), sem(n("angle_ready")), sem(n("sin_ready"))
                L.factor_step, L.factors_ready, L.z1_ready = sem(n("factor_step")), sem(n("factors_ready")), sem(n("z1_ready"))
            return L

        nodes = [node_layer(0), node_layer(1)]

        def group(dram, turn, w):
            return dram[0:NODES, :].rearrange("(g p j) w -> g p (j w)", p=P, j=J)[turn.n]

        block = ctx.enter_context(nc.Block())

        def zero_part(sp, k, i):
            w = TABLE * (OUT0, OUT1)[k] // P // ZERO_DMAS[k]
            parts = (sums0, sums1)[k].rearrange("r w -> (r w)").rearrange("(n p w) -> n p w", p=P, w=w)
            sp.dma_start(parts[i], zeros[:, 0:w]).then_inc((s_zeroed0, s_zeroed1)[k], 16)

        def sync_edges(sp, L):
            if L.k == 0:
                sp.wait_ge(s_unit_stored, 16)

            def turn(s):
                if L.k == 0 and not isinstance(s.i, int):
                    zero_part(sp, 1, s.n - 4)
                if L.k == 0 and isinstance(s.i, int) and -4 < s.n < 0:
                    zero_part(sp, 0, ZERO_DMAS[0] + s.n)
                t = s.plus(4)
                if t.exists:
                    b = t.slot(2)
                    if t.back(2):
                        sp.wait_ge(L.gathered[b], 32 * t.round)
                    sp.dma_start(L.gidx[b][:, :], L.gather_key[:, bass.ds(2 * t.n, 2)]).then_inc(L.gidx_loaded[b], 16)
                t = s.plus(3)
                if t.exists:
                    b = t.slot(2)
                    if t.back(2):
                        sp.wait_ge(L.features_up, t.n - 1)
                    sp.dma_start(L.hid[b][:, :], L.hidden_dram[:, bass.ds(2 * TILE * t.n, 2 * TILE)]).then_inc(L.hidden_loaded[b], 16)
                t = s.plus(2)
                if t.exists:
                    b = t.slot(2)
                    if t.back(2):
                        sp.wait_ge(L.same_ready, t.n - 1)
                    sp.dma_start(L.kcol[b][:, :], L.key_cols[:, bass.ds(2 * t.n, 2)]).then_inc(L.keys_loaded[b], 16)
                    sp.dma_start(L.krow[b][:, :], L.key_rows[bass.ds(t.n, 1), :].to_broadcast((P, 2 * TILE))).then_inc(L.keys_loaded[b], 16)
                    if t.back(2):
                        sp.wait_ge(L.msg_ready, t.n - 1)
                    sp.dma_start(L.geom[b][:, :, :].rearrange("p a g -> p (a g)"),
                                 L.geo_dram[:, bass.ds(2 * L.geo * t.n, 2 * L.geo)]).then_inc(L.geom_loaded[b], 16)

            run_turns(sp, PAIRS, 2, 4, 1, turn)

        def sync_nodes(sp, L):
            def turn(s):
                t = s.plus(6)
                if t.exists:
                    b = t.slot(RING)
                    if t.back(RING):
                        sp.wait_ge(L.y_ready, t.n - RING + 1)
                        if L.k == 0:
                            sp.wait_ge(L.t_ready, t.n - RING + 1)
                            sp.wait_ge(L.attr_copied, t.n - RING + 1)
                    sp.dma_start(L.x[b].rearrange("p j w -> p (j w)"), group(L.x_dram, t, ROW)).then_inc(L.x_loaded[b], 16)
                    sp.dma_start(L.agg_flat[b], group(L.sums, t, L.sums_w)).then_inc(L.sums_loaded[b], 16)
                t = s.plus(-3)
                if t.exists:
                    b = t.slot(HALF_RING)
                    sp.wait_ge(L.norm_ready, t.n + 1)
                    if L.k == 0:
                        sp.wait_ge(L.attr_copied, t.n + 1)
                    sp.dma_start(group(L.out_dram, t, L.out_w), L.res_flat[b]).then_inc(L.stored[b], 16)

            run_turns(sp, GROUPS, RING, 6, 3, turn)

        def wait_stored(engine, L):
            for b in range(HALF_RING):
                engine.wait_ge(L.stored[b], 16 * len(range(b, GROUPS, HALF_RING)))

        @block.sync
        def _(sp):
            sp.dma_start(vec[:, :, :].rearrange("p t c -> p (t c)"), t_in["edge_vec"]).then_inc(s_setup, 16)
            for n in wt:
                sp.dma_start(wt[n][:, :], t_in[n]).then_inc(s_setup, 16)
            sp.wait_ge(s_zero_tile, 1)
            with sp.Fori(0, ZERO_DMAS[0] - 3) as i:
                zero_part(sp, 0, i)
            sp.wait_ge(s_unit, 1)
            sp.dma_start(unit_rows, unit[:, :, :].rearrange("p t c -> p (t c)")).then_inc(s_unit_stored, 16)
            sync_edges(sp, layers[0])
            for i in range(LOOPED, ZERO_DMAS[1]):
                zero_part(sp, 1, i)
            for b in range(2):
                sp.wait_ge(layers[0].scattered[b], 32 * (PAIRS // 2))
            sync_nodes(sp, nodes[0])
            wait_stored(sp, nodes[0])
            sync_edges(sp, layers[1])
            for b in range(2):
                sp.wait_ge(layers[1].scattered[b], 32 * (PAIRS // 2))
            sync_nodes(sp, nodes[1])
            wait_stored(sp, nodes[1])

        def pool_edges(pool, L):
            def turn(s):
                t = s.plus(3)
                if t.exists:
                    b = t.slot(2)
                    if t.back(2):
                        pool.wait_ge(L.features_up, t.n - 1)
                        if L.k == 1:
                            pool.wait_ge(L.lhs_ready, t.n - 1)
                    wait_apart(pool, L.gidx_loaded[b], 16 * (t.round + 1))
                    for a in range(2):
                        nc.gpsimd.indirect_dma_start(
                            L.got[b][:, a, S:S + ROW], None, L.rows, bass.IndirectOffsetOnAxis(ap=L.gidx[b][:, a:a + 1], axis=0)
                        ).then_inc(L.gathered[b], 16)
                t = s.plus(-1)
                if t.exists:
                    b = t.slot(2)
                    pool.wait_ge(L.acc_ready, t.n + 1)
                    pool.wait_ge(L.sidx_ready, t.n + 1)
                    if t.back(1):
                        u = t.plus(-1)
                        wait_apart(pool, L.scattered[u.slot(2)], 32 * (u.round + 1))
                    else:
                        pool.wait_ge(L.zeroed, 16 * L.zero_dmas)
                    for a in range(2):
                        nc.gpsimd.indirect_dma_start(
                            L.sums, bass.IndirectOffsetOnAxis(ap=L.sidx[b][:, a:a + 1], axis=0), L.acc[b][:, a, :], None,
                            bounds_check=TABLE - 1, oob_is_err=True, compute_op=ALU.add,
                        ).then_inc(L.scattered[b], 16)

            run_turns(pool, PAIRS, 2, 4, 1, turn)

        def pool_rstd(pool, L, t):
            b = t.slot(2)
            gp = nc.gpsimd
            if L.k == 1:
                wait_apart(pool, L.mv_ready, t.n + 1)
                gp.tensor_scalar(node_varp[b][:, :], node_mv[b][:, :, 1], EPS, None, ALU.add).then_inc(L.varp_ready, 1)
            pool.wait_ge(L.varp_ready, t.n + 1)
            if t.back(2):
                pool.wait_ge(L.norm_ready, t.n - 1)
            gp.tensor_tensor(node_rstd[b][:, :], node_varp[b][:, :], minus_half[:, 0:J], ALU.pow).then_inc(L.rstd_ready, 1)
            if L.k == 1:
                pool.wait_ge(L.rstd_ready, t.n + 1)
                gp.tensor_tensor(node_meanr[:, :], node_mv[b][:, :, 0], node_rstd[b][:, :], ALU.mult).then_inc(L.meanr_ready, 1)
                wait_apart(pool, L.meanr_ready, t.n + 1)
                gp.tensor_scalar(node_shift[b][:, :], node_meanr[:, :], -1.0, None, ALU.mult).then_inc(L.shift_ready, 1)

        def pool_nodes0(pool, L):
            gp = nc.gpsimd

            def turn(s):
                t = s.plus(-2)
                if t.exists:
                    pool_rstd(pool, L, t)
                t = s
                if t.exists:
                    b, b8 = t.slot(HALF_RING), t.slot(RING)
                    if t.back(HALF_RING):
                        pool.wait_ge(L.stored[b], 16 * t.half_round)
                    wait_apart(pool, L.x_loaded[b8], 16 * (t.round + 1))
                    gp.tensor_copy(L.res[b][:, :, D:ROW], L.x[b8][:, :, D:ROW]).then_inc(L.attr_copied, 1)
                    pool.wait_ge(L.silu_ready, t.n + 1)
                    pool.wait_ge(L.gated_ready, t.n + 1)
                    gp.tensor_tensor(node_y[b][:, :, :], node_y[b][:, :, :], L.x[b8][:, :, 0:D], ALU.add).then_inc(L.y_ready, 1)

            run_turns(pool, GROUPS, RING, 4, 3, turn)

        TWO_PI = [6.28125, 0.0019350051879882812, 3.0199159819567e-07]
        ROUNDER = 12582912.0
        ANGLE_STEPS, FACTOR_STEPS = 9, 2

        def pool_nodes1(pool, L):
            gp = nc.gpsimd

            def angles(t, h):
                done = [0]

                def step(ins):
                    done[0] += 1
                    ins.then_inc(L.angle_step, 1)
                    wait_apart(pool, L.angle_step, ANGLE_STEPS * h.n + done[0])

                b = t.slot(RING)
                for g in range(2):
                    pool.wait_ge(L.x_loaded[b + g], 16 * (t.round + 1))
                    pool.wait_ge(L.sums_loaded[b + g], 16 * (t.round + 1))
                step(gp.tensor_tensor(angle[:, :, :], L.agg_ring[:, b:b + 2, :, 0], node_x[:, b:b + 2, :, D], ALU.mult))
                step(gp.tensor_scalar(turns[:, :, :], angle[:, :, :], 0.15915494309189535, ROUNDER, ALU.mult, ALU.add))
                step(gp.tensor_scalar(turns[:, :, :], turns[:, :, :], ROUNDER, None, ALU.subtract))
                left = angle
                for c in TWO_PI:
                    step(gp.tensor_scalar(part[:, :, :], turns[:, :, :], c, None, ALU.mult))
                    step(gp.tensor_tensor(rest[:, :, :], left[:, :, :], part[:, :, :], ALU.subtract))
                    left = rest
                if h.back(1):
                    wait_apart(pool, L.sin_ready, h.n)
                gp.tensor_scalar(reduced[:, :], rest[:, :, :].rearrange("p g j -> p (g j)"), 3.1415925, -3.1415925,
                                 ALU.min, ALU.max).then_inc(L.angle_ready, 1)

            def factors(t, h):
                b, b8 = h.slot(HALF_RING), t.slot(RING)
                done = [0]

                def step(ins):
                    done[0] += 1
                    ins.then_inc(L.factor_step, 1)
                    wait_apart(pool, L.factor_step, FACTOR_STEPS * h.n + done[0])

                pool.wait_ge(L.sin_ready, h.n + 1)
                step(gp.tensor_tensor(square[:, :, :], half_sine[:, :, :], half_sine[:, :, :], ALU.mult))
                step(gp.tensor_scalar(cosine[:, :, :], square[:, :, :], -2.0, 1.0, ALU.mult, ALU.add))
                if h.back(HALF_RING):
                    pool.wait_ge(L.y_ready, t.n - 6)
                attr = node_x[:, b8:b8 + 2, :, D]
                gp.tensor_tensor(by_sin[b][:, :, :], sine[:, :, :], attr, ALU.mult)
                gp.tensor_tensor(by_cos[b][:, :, :], cosine[:, :, :], attr, ALU.mult).then_inc(L.factors_ready, 1)

            def turn(s):
                t = s.plus(-2)
                if t.exists:
                    pool_rstd(pool, L, t)
                if s.offset % 2 == 0:
                    t = s.plus(4)
                    if t.exists:
                        angles(t, t.halved)
                else:
                    t = s.plus(3)
                    if t.exists:
                        factors(t, t.halved)

            run_turns(pool, GROUPS, RING, 4, 3, turn)

        @block.gpsimd
        def _(pool):
            gp = nc.gpsimd
            gp.memset(zeros[:, :], 0.0).then_inc(s_zero_tile, 1)
            gp.memset(minus_half[:, :], -0.5)
            gp.memset(ident[:, :], 0.0).then_inc(s_pool_const, 1)
            gp.memset(earlier[:, :, :], 1.0).then_inc(s_pool_const, 1)
            pool.wait_ge(s_pool_const, 2)
            gp.affine_select(out=ident[:, :], in_=ident[:, :], compare_op=ALU.not_equal, fill=1.0, base=0,
                             pattern=[[-1, P]], channel_multiplier=1).then_inc(s_pool_const, 1)
            for a in range(2):
                gp.affine_select(out=earlier[:, a, :], in_=earlier[:, a, :], compare_op=ALU.is_gt, fill=0.0, base=TILE * a,
                                 pattern=[[-1, 2 * TILE]], channel_multiplier=1).then_inc(s_pool_const, 1)
            gp.iota(spare_i[:, :], pattern=[[TILE, 2]], base=NODES, channel_multiplier=1).then_inc(s_spare, 1)
            pool.wait_ge(s_spare, 1)
            gp.tensor_copy(spare[:, :], spare_i[:, :]).then_inc(s_pool_const, 1)
            pool.wait_ge(s_pool_const, 6)
            pool.wait_ge(s_vec_n, 1)
            gp.tensor_tensor(vec_r[:, :], vec_n[:, :], minus_half[:, :], ALU.pow).then_inc(s_vec_r, 1)
            pool_edges(pool, layers[0])
            pool_nodes0(pool, nodes[0])
            wait_stored(pool, nodes[0])
            pool_edges(pool, layers[1])
            pool_nodes1(pool, nodes[1])

        def pe_edges(pe, L):
            mm = nc.tensor.matmul
            fc1, fc2_in_s, in_v = (wt["%s_%d" % (n, L.k)] for n in ("fc1", "fc2_in_s", "in_v"))
            end = L.w + S
            PT = pPT[:, 0:2 * 512].rearrange("p (a n e) -> p a n e", a=2, e=TILE)
            M = pM[:, 0:448].rearrange("p (a w) -> p a w", a=2)
            C = pC[:, 0:2 * L.out].rearrange("p (a w) -> p a w", a=2)

            def turn(s):
                t = s.plus(1)
                if t.exists:
                    pe.wait_ge(L.lhs_ready, t.n + 1)
                    if t.back(1):
                        pe.wait_ge(L.products_ready, t.n)
                    for a in range(2):
                        e = bass.ds(a * TILE, TILE)
                        mm(pWX[:, a, 0:end], L.hsT[:, e], fc2_in_s[:, :], start=True, stop=True)
                        last = mm(pWX[:, a, end:end + L.xv], L.xvT[:, a, :], in_v[:, :], start=True, stop=True)
                    last.then_inc(L.wx_done, 1)
                t = s
                if t.exists:
                    pe.wait_ge(L.products_ready, t.n + 1)
                    if t.back(1):
                        pe.wait_ge(L.pt_ready, t.n)
                    for a in range(2):
                        for n, (c, w) in enumerate(L.blocks):
                            last = nc.tensor.transpose(PT[0:w, a, n, :], L.prod[:, a, c:c + w], ident[:, :])
                    last.then_inc(L.pt_done, 1)
                t = s.plus(-1)
                if t.exists:
                    b = t.slot(2)
                    pe.wait_ge(L.msg_ready, t.n + 1)
                    pe.wait_ge(L.same_ready, t.n + 1)
                    if t.back(1):
                        pe.wait_ge(L.acc_ready, t.n)
                    mm(C[:, 0, :], L.same[b][:, 0, 0:TILE], L.msg[:, 0, :], start=True, stop=False)
                    mm(C[:, 0, :], L.same[b][:, 1, 0:TILE], L.msg[:, 1, :], start=False, stop=True)
                    last = mm(C[:, 1, :], L.same[b][:, 1, TILE:2 * TILE], L.msg[:, 1, :], start=True, stop=True)
                    last.then_inc(L.c_done, 1)
                t = s.plus(2)
                if t.exists:
                    b = t.slot(2)
                    if t.back(1):
                        pe.wait_ge(L.lhs_ready, t.n)
                    pe.wait_ge(L.gathered[b], 32 * (t.round + 1))
                    wait_apart(pe, L.hidden_loaded[b], 16 * (t.round + 1))
                    mm(pH[0:S, :], fc1[:, :], L.hid[b][:, :], start=True, stop=True)
                    for a in range(2):
                        nc.tensor.transpose(pXT[:, a * TILE:(a + 1) * TILE], L.got[b][:, a, 0:2 * S], ident[:, :])
                        last = nc.tensor.transpose(pXT[0:V3, (2 + a) * TILE:(3 + a) * TILE], L.got[b][:, a, 2 * S:S + D], ident[:, :])
                    last.then_inc(L.features_up, 1)
                t = s
                if t.exists:
                    pe.wait_ge(L.pt_ready, t.n + 1)
                    if t.back(1):
                        pe.wait_ge(L.msg_ready, t.n)
                    for a in range(2):
                        mm(M[:, a, 0:L.sa_w], L.pT[:, a, 0, :], wt["out_sa_%d" % L.k][:, :], start=True, stop=False)
                        if L.k == 0:
                            mm(M[:, a, 128:224], L.pT[0:V3, a, 2, :], wt["out_b_0"][:, :], start=False, stop=False)
                        last = mm(M[:, a, V:V + L.out], L.pT[:, a, 1, :], wt["out_dc_0" if L.k == 0 else "out_db_1"][:, :],
                                  start=False, stop=True)
                    last.then_inc(L.m_done, 1)

            run_turns(pe, PAIRS, 2, 4, 1, turn)

        xt_psum = [wide[0], wide[1]]
        o_psum = [[bank[0], bank[1]], [bank[2], bank[3]]]

        def pe_nodes(pe, L):
            mm = nc.tensor.matmul
            ws, wv = wt["skip_s_%d" % L.k], wt["skip_v_%d" % L.k]
            so = 96 if L.k == 0 else S

            def turn(s):
                t = s.plus(2)
                if t.exists:
                    b, b8 = t.slot(2), t.slot(RING)
                    xt = xt_psum[b]
                    pe.wait_ge(L.x_loaded[b8], 16 * (t.round + 1))
                    if t.back(2):
                        wait_apart(pe, L.xt_ready, t.n - 1)
                    for j in range(J):
                        nc.tensor.transpose(xt[0:S, j * P:(j + 1) * P], L.x[b8][:, j, 0:S], ident[:, :])
                        last = nc.tensor.transpose(xt[0:V3, (J + j) * P:(J + j + 1) * P], L.x[b8][:, j, S:D], ident[:, :])
                    last.then_inc(L.xt_done, 1)
                t = s.plus(1)
                if t.exists:
                    b = t.slot(2)
                    pe.wait_ge(L.xt_ready, t.n + 1)
                    if t.back(2):
                        pe.wait_ge(L.t_ready if L.k == 0 else L.z1_ready, t.n - 1)
                    for j in range(J):
                        o = o_psum[b][j // 2][:, (j % 2) * 256:(j % 2 + 1) * 256]
                        mm(o[:, 0:ws.shape[1]], node_xsT[b][:, j, :], ws[:, :], start=True, stop=True)
                        last = mm(o[:, so:so + V3], node_xvT[b][:, j, :], wv[:, :], start=True, stop=True)
                    last.then_inc(L.o_done, 1)

            run_turns(pe, GROUPS, RING, 4, 3, turn)

        def pe_warm(pe, L):
            for b in range(2):
                pe.wait_ge(L.scattered[b], 32 * (PAIRS // 2))
            for _ in range(WARM_PRODUCTS):
                nc.tensor.matmul(bank[0][:, :], ident[:, :], earlier[:, :, :].rearrange("p a e -> p (a e)"), start=True, stop=True)

        @block.tensor
        def _(pe):
            pe.wait_ge(s_pool_const, 6)
            pe.wait_ge(s_scaled, 1)
            pe.wait_ge(s_zeros, 1)
            for k in range(2):
                pe_edges(pe, layers[k])
                pe_warm(pe, layers[k])
                pe_nodes(pe, nodes[k])

        def act_edges(act, L):
            X = pWX[:, :, L.w:L.w + L.x]
            PT = pPT[:, 0:2 * 512].rearrange("p (a n e) -> p a (n e)", a=2, e=TILE)
            M = pM[:, 0:448].rearrange("p (a w) -> p a w", a=2)
            copy, cp = nc.scalar.activation, ACT.Copy

            def turn(s):
                t = s.plus(1)
                if t.exists:
                    act.wait_ge(L.wx_done, t.n + 1)
                    if t.back(1):
                        act.wait_ge(L.products_ready, t.n)
                    copy(L.xs[:, :, :], X, cp).then_inc(L.x_ready, 1)
                t = s
                if t.exists:
                    act.wait_ge(L.pt_done, t.n + 1)
                    if t.back(1):
                        act.wait_ge(L.m_done, t.n)
                    last = copy(L.pT[:, :, 0:2, :].rearrange("p a n e -> p a (n e)"), PT[:, :, 0:2 * TILE], cp)
                    if L.k == 0:
                        last = copy(L.pT[0:V3, :, 2, :], PT[0:V3, :, 2 * TILE:3 * TILE], cp)
                    last.then_inc(L.pt_ready, 1)
                t = s.plus(-1)
                if t.exists:
                    b = t.slot(2)
                    act.wait_ge(L.c_done, t.n + 1)
                    if t.back(2):
                        act.wait_ge(L.scattered[b], 32 * t.round)
                    copy(L.acc[b][:, :, :].rearrange("p a w -> p (a w)"), pC[:, 0:2 * L.out], cp).then_inc(L.acc_ready, 1)
                t = s.plus(2)
                if t.exists:
                    b = t.slot(2)
                    act.wait_ge(L.features_up, t.n + 1)
                    if t.back(1):
                        act.wait_ge(L.wx_done, t.n)
                    if L.k == 0:
                        copy(L.hsT[0:S, :], pH[0:S, :], ACT.Relu)
                    else:
                        copy(L.hsT[0:S, :], pH[0:S, :], ACT.Silu, scale=8.0 ** -0.5)
                        if t.back(1):
                            act.wait_ge(L.geo_ready, t.n)
                        copy(L.attr[:, :], L.got[b][:, :, S + D], cp)
                    copy(L.hsT[S:2 * S, :], pXT[S:2 * S, 0:2 * TILE], cp)
                    copy(L.xvT[:, :, :].rearrange("p a e -> p (a e)"), pXT[0:V3, 2 * TILE:4 * TILE], cp).then_inc(L.lhs_ready, 1)

            run_turns(act, PAIRS, 2, 4, 1, turn)

        def act_nodes(act, L):
            f = nc.scalar.activation

            def turn(s):
                t = s
                if t.exists and L.k == 0:
                    b, b4 = t.slot(2), t.slot(HALF_RING)
                    act.wait_ge(L.t_ready, t.n + 1)
                    if t.back(2):
                        act.wait_ge(L.gated_ready, t.n - 1)
                    f(node_gate[b][:, :, :], node_t[b][:, :, S:96], ACT.Tanh, scale=0.5).then_inc(L.tanh_ready, 1)
                    if t.back(HALF_RING):
                        act.wait_ge(L.norm_ready, t.n - 3)
                    f(node_y[b4][:, :, 0:S], node_t[b][:, :, 0:S], ACT.Silu).then_inc(L.silu_ready, 1)
                t = s.plus(2)
                if t.exists:
                    b = t.slot(2)
                    act.wait_ge(L.xt_done, t.n + 1)
                    if t.back(2):
                        act.wait_ge(L.o_done, t.n - 1)
                    f(node_xsT[b][:, :, :].rearrange("p n e -> p (n e)"), xt_psum[b][0:S, 0:512], ACT.Copy)
                    f(node_xvT[b][:, :, :].rearrange("p n e -> p (n e)"), xt_psum[b][0:V3, 512:1024], ACT.Copy).then_inc(L.xt_ready, 1)
                t = s.plus(-3)
                if t.exists:
                    b, b4 = t.slot(2), t.slot(HALF_RING)
                    act.wait_ge(L.shift_ready, t.n + 1)
                    if t.back(HALF_RING):
                        act.wait_ge(L.stored[b4], 16 * t.half_round)
                    for j in range(J):
                        last = f(L.res[b4][:, j, 0:D], node_y[b4][:, j, :], ACT.Identity,
                                 bias=node_shift[b][:, j:j + 1], scale=node_rstd[b][:, j:j + 1])
                    last.then_inc(L.norm_ready, 1)
                t = s.plus(4)
                if L.k == 1 and s.offset % 2 == 0 and t.exists:
                    h = t.halved
                    act.wait_ge(L.angle_ready, h.n + 1)
                    if h.back(1):
                        act.wait_ge(L.factors_ready, h.n)
                    f(sine[:, :, :].rearrange("p g j -> p (g j)"), reduced[:, :], ACT.Sin)
                    f(half_sine[:, :, :].rearrange("p g j -> p (g j)"), reduced[:, :], ACT.Sin, scale=0.5).then_inc(L.sin_ready, 1)

            run_turns(act, GROUPS, RING, 4, 3, turn)

        @block.scalar
        def _(act):
            act.wait_ge(s_setup, 16 * (1 + len(wt)))
            for n, lo, hi, c in weight_scale:
                last = nc.scalar.activation(wt[n][:, lo:hi], wt[n][:, lo:hi], ACT.Copy, scale=float(c))
            last.then_inc(s_scaled, 1)
            act_edges(act, layers[0])
            act_nodes(act, nodes[0])
            act_edges(act, layers[1])
            act_nodes(act, nodes[1])

        def dve_edges(dve, L):
            v = nc.vector
            W = pWX[:, :, 0:L.w]
            M = pM[:, 0:448].rearrange("p (a w) -> p a w", a=2)
            vo = L.vo

            def vec3(x):
                return x.rearrange("p a (m c) -> p a m c", c=3)

            def over3(x):
                return x.unsqueeze(3).to_broadcast((P, 2, V, 3))

            def geo(g, c):
                return g[:, :, c:c + 3].unsqueeze(2).to_broadcast((P, 2, V, 3))

            def turn(s):
                t = s
                if t.exists:
                    b = t.slot(2)
                    dve.wait_ge(L.keys_loaded[b], 32 * (t.round + 1))
                    v.tensor_copy(L.key[:, :], L.kcol[b][:, :]).then_inc(L.key_ready, 1)
                    dve.wait_ge(L.key_ready, t.n + 1)
                    for a in range(2):
                        cols = (a + 1) * TILE
                        last = v.scalar_tensor_tensor(L.junk[:, a, 0:cols], L.krow[b][:, 0:cols], L.key[:, a:a + 1],
                                                      earlier[:, a, 0:cols], ALU.is_equal, ALU.mult, accum_out=L.before[:, a:a + 1])
                    last.then_inc(L.before_ready, 1)
                    v.tensor_tensor(L.away[:, :], spare[:, :], L.key[:, :], ALU.subtract).then_inc(L.away_ready, 1)
                    if t.back(2):
                        dve.wait_ge(L.c_done, t.n - 1)
                    for a in range(2):
                        cols = (a + 1) * TILE
                        last = v.tensor_scalar(L.same[b][:, a, 0:cols], L.krow[b][:, 0:cols], L.key[:, a:a + 1], None, ALU.is_equal)
                        if a == 0:
                            dve.wait_ge(L.before_ready, t.n + 1)
                            dve.wait_ge(L.away_ready, t.n + 1)
                            v.scalar_tensor_tensor(L.move[:, :], L.before[:, :], 1.0, L.away[:, :], ALU.min, ALU.mult).then_inc(L.move_ready, 1)
                    last.then_inc(L.same_ready, 1)
                    dve.wait_ge(L.move_ready, t.n + 1)
                    if t.back(2):
                        dve.wait_ge(L.scattered[b], 32 * t.round)
                    v.tensor_tensor(L.sidx[b][:, :], L.move[:, :], L.key[:, :], ALU.add).then_inc(L.sidx_ready, 1)
                t = s.plus(1)
                if t.exists:
                    b = t.slot(2)
                    dve.wait_ge(L.geom_loaded[b], 16 * (t.round + 1))
                    if L.k == 1:
                        dve.wait_ge(L.lhs_ready, t.n + 1)
                        v.tensor_tensor(L.geo_s[b][:, :, :], L.geom[b][:, :, :],
                                        L.attr[:, :].unsqueeze(2).to_broadcast((P, 2, 4)), ALU.mult).then_inc(L.geo_ready, 1)
                        dve.wait_ge(L.geo_ready, t.n + 1)
                    dve.wait_ge(L.x_ready, t.n + 1)
                    if t.back(1):
                        dve.wait_ge(L.pt_done, t.n)
                    xs = L.xs[:, :, 0:S]
                    g = L.geom[b] if L.k == 0 else L.geo_s[b]
                    if L.k == 0:
                        xv = L.xs[:, :, S:S + 160].rearrange("p a (m c) -> p a m c", c=5)
                        v.tensor_tensor(vec3(L.t0[:, :, :]), xv[:, :, :, 0:3], geo(g, 0), ALU.mult).then_inc(L.t0_ready, 1)
                        v.tensor_tensor(vec3(L.t1[:, :, :]), xv[:, :, :, 1:4], geo(g, 2), ALU.mult)
                        v.tensor_tensor(vec3(L.t2[:, :, :]), xv[:, :, :, 2:5], geo(g, 1), ALU.mult).then_inc(L.cross_parts, 1)
                        dve.wait_ge(L.t0_ready, t.n + 1)
                        v.tensor_reduce(L.dot[:, :, :], vec3(L.t0[:, :, :]), AX.X, ALU.add).then_inc(L.dot_ready, 1)
                        dve.wait_ge(L.cross_parts, t.n + 1)
                        v.tensor_tensor(L.cross[:, :, :], L.t1[:, :, :], L.t2[:, :, :], ALU.subtract).then_inc(L.cross_ready, 1)
                        v.tensor_tensor(L.prod[:, :, 0:2 * S].rearrange("p a (n c) -> p a n c", c=S), W[:, :, 0:2 * S].rearrange("p a (n c) -> p a n c", c=S),
                                        xs.unsqueeze(2).to_broadcast((P, 2, 2, S)), ALU.mult)
                        v.tensor_tensor(vec3(L.prod[:, :, 256:352]), over3(W[:, :, 128:160]), xv[:, :, :, 0:3], ALU.mult)
                        dve.wait_ge(L.dot_ready, t.n + 1)
                        v.tensor_tensor(L.prod[:, :, 128:160], W[:, :, 160:192], L.dot[:, :, :], ALU.mult)
                        dve.wait_ge(L.cross_ready, t.n + 1)
                        v.tensor_tensor(vec3(L.prod[:, :, 160:256]), over3(W[:, :, 192:224]), vec3(L.cross[:, :, :]),
                                        ALU.mult).then_inc(L.products_ready, 1)
                    else:
                        xv = vec3(L.xs[:, :, S:D])
                        v.tensor_tensor(vec3(L.t0[:, :, :]), xv, geo(g, 1), ALU.mult).then_inc(L.t0_ready, 1)
                        for a in range(2):
                            v.scalar_tensor_tensor(L.prod[:, a, 0:S], W[:, a, 0:S], g[:, a, 0:1], xs[:, a, :], ALU.mult, ALU.mult)
                            v.scalar_tensor_tensor(vec3(L.prod[:, :, 160:256])[:, a], W[:, a, 128:160].unsqueeze(2).to_broadcast((P, V, 3)),
                                                   g[:, a, 0:1], xv[:, a], ALU.mult, ALU.mult)
                        dve.wait_ge(L.t0_ready, t.n + 1)
                        v.tensor_reduce(L.dot[:, :, :], vec3(L.t0[:, :, :]), AX.X, ALU.add).then_inc(L.dot_ready, 1)
                        v.tensor_tensor(L.prod[:, :, S:2 * S], W[:, :, S:2 * S], xs, ALU.mult)
                        dve.wait_ge(L.dot_ready, t.n + 1)
                        v.tensor_tensor(L.prod[:, :, 128:160], W[:, :, 160:192], L.dot[:, :, :], ALU.mult).then_inc(L.products_ready, 1)
                t = s
                if t.exists:
                    b = t.slot(2)
                    g, c = (L.geom[b], 0) if L.k == 0 else (L.geo_s[b], 1)
                    dve.wait_ge(L.m_done, t.n + 1)
                    v.tensor_tensor(vec3(L.outer[:, :, vo:vo + V3]), over3(M[:, :, 0:V]), geo(g, c), ALU.mult).then_inc(L.outer_ready, 1)
                    dve.wait_ge(L.outer_ready, t.n + 1)
                    if t.back(1):
                        dve.wait_ge(L.c_done, t.n)
                    v.tensor_tensor(L.msg[:, :, :], M[:, :, V:V + L.out], L.outer[:, :, :], ALU.add).then_inc(L.msg_ready, 1)

            run_turns(dve, PAIRS, 2, 4, 1, turn)

        def dve_stats(dve, L, t):
            dve.wait_ge(L.y_ready, t.n + 1)
            if t.back(1):
                dve.wait_ge(L.mv_ready, t.n)
            for j in range(J):
                last = nc.vector.bn_stats(node_stats[:, j, :], node_y[t.slot(HALF_RING)][:, j, :])
            last.then_inc(L.stats_ready, 1)

        def dve_norm(dve, L, s):
            v = nc.vector
            t = s.plus(-1)
            if t.exists:
                b = t.slot(2)
                if L.k == 1 and t.back(2):
                    wait_apart(dve, L.meanr_ready, t.n - 1)
                wait_apart(dve, L.stats_ready, t.n + 1)
                for j in range(J):
                    last = v.bn_aggr(node_mv[b][:, j, :], node_stats[:, j, :])
                last.then_inc(L.mv_ready, 1)
            if L.k == 1:
                return
            t = s.plus(-2)
            if t.exists:
                b = t.slot(2)
                dve.wait_ge(L.rstd_ready, t.n + 1)
                if t.back(2):
                    dve.wait_ge(L.norm_ready, t.n - 1)
                v.scalar_tensor_tensor(node_shift[b][:, :], node_mv[b][:, :, 0], -1.0, node_rstd[b][:, :],
                                       ALU.mult, ALU.mult).then_inc(L.shift_ready, 1)
            t = s.plus(-1)
            if t.exists:
                b = t.slot(2)
                dve.wait_ge(L.mv_ready, t.n + 1)
                if t.back(2):
                    dve.wait_ge(L.rstd_ready, t.n - 1)
                v.tensor_scalar(node_varp[b][:, :], node_mv[b][:, :, 1], EPS, None, ALU.add).then_inc(L.varp_ready, 1)

        def dve_nodes0(dve, L):
            v = nc.vector

            def turn(s):
                t = s
                if t.exists:
                    b, b4 = t.slot(2), t.slot(HALF_RING)
                    dve.wait_ge(L.tanh_ready, t.n + 1)
                    if t.back(HALF_RING):
                        dve.wait_ge(L.norm_ready, t.n - 3)
                    v.scalar_tensor_tensor(node_y[b4][:, :, S:D].rearrange("p j (m c) -> p j m c", c=3),
                                           node_gate[b][:, :, :].unsqueeze(3).to_broadcast((P, J, V, 3)), 1.0,
                                           node_t[b][:, :, 96:192].rearrange("p j (m c) -> p j m c", c=3),
                                           ALU.add, ALU.mult).then_inc(L.gated_ready, 1)
                t = s.plus(-1)
                if t.exists:
                    dve_stats(dve, L, t)
                t = s.plus(1)
                if t.exists:
                    b, b8 = t.slot(2), t.slot(RING)
                    dve.wait_ge(L.sums_loaded[b8], 16 * (t.round + 1))
                    dve.wait_ge(L.o_done, t.n + 1)
                    if t.back(2):
                        dve.wait_ge(L.silu_ready, t.n - 1)
                        dve.wait_ge(L.gated_ready, t.n - 1)
                    for h in range(2):
                        o = o_psum[b][h][:, :].rearrange("p (j w) -> p j w", w=256)[:, :, 0:OUT0]
                        last = v.tensor_tensor(node_t[b][:, 2 * h:2 * h + 2, :], o, L.agg[b8][:, 2 * h:2 * h + 2, :], ALU.add)
                    last.then_inc(L.t_ready, 1)
                dve_norm(dve, L, s)

            run_turns(dve, GROUPS, RING, 4, 3, turn)

        def dve_nodes1(dve, L):
            v = nc.vector

            def turn(s):
                t = s
                if t.exists:
                    b, b4, b8 = t.slot(2), t.slot(HALF_RING), t.slot(RING)
                    h = t.halved
                    fc, fs = (x[h.slot(HALF_RING)][:, t.offset % 2, :] for x in (by_cos, by_sin))
                    dve.wait_ge(L.o_done, t.n + 1)
                    dve.wait_ge(L.factors_ready, h.n + 1)
                    if t.back(HALF_RING):
                        dve.wait_ge(L.norm_ready, t.n - 3)
                    for j in range(J):
                        o = o_psum[b][j // 2][:, (j % 2) * 256:(j % 2) * 256 + D]
                        last = v.scalar_tensor_tensor(node_y[b4][:, j, :], o, fc[:, j:j + 1], L.x[b8][:, j, 0:D], ALU.mult, ALU.add)
                    last.then_inc(L.z1_ready, 1)
                if s.plus(-1).exists:
                    dve_stats(dve, L, s.plus(-1))
                if t.exists:
                    dve.wait_ge(L.z1_ready, t.n + 1)
                    for j in range(J):
                        last = v.scalar_tensor_tensor(node_y[b4][:, j, :], L.agg[b8][:, j, 1:OUT1], fs[:, j:j + 1], node_y[b4][:, j, :],
                                                      ALU.mult, ALU.add)
                    last.then_inc(L.y_ready, 1)
                dve_norm(dve, L, s)

            run_turns(dve, GROUPS, RING, 4, 3, turn)

        @block.vector
        def _(dve):
            v = nc.vector
            dve.wait_ge(s_setup, 16 * (1 + len(wt)))
            v.tensor_tensor(vec_sq[:, :, :], vec[:, :, :], vec[:, :, :], ALU.mult).then_inc(s_vec_sq, 1)
            dve.wait_ge(s_vec_sq, 1)
            v.tensor_reduce(vec_n[:, :], vec_sq[:, :, :], AX.X, ALU.add).then_inc(s_vec_n, 1)
            dve.wait_ge(s_vec_r, 1)
            for lo, n in ((0, 3), (3, 2)):
                last = v.tensor_tensor(unit[:, :, lo:lo + n], vec[:, :, 0:n],
                                       vec_r[:, :].unsqueeze(2).to_broadcast((P, 2 * PAIRS, n)), ALU.mult)
            last.then_inc(s_unit, 1)
            dve.wait_ge(s_pool_const, 6)
            for L in layers:
                for b in range(2):
                    v.memset(L.got[b][:, :, 0:S], 0.0)
                last = v.memset(L.outer[:, :, :], 0.0)
            last.then_inc(s_zeros, 1)
            dve.wait_ge(s_zeros, 1)
            dve_edges(dve, layers[0])
            dve_nodes0(dve, nodes[0])
            dve_edges(dve, layers[1])
            dve_nodes1(dve, nodes[1])


def kernel(x, src, dst, edge_attr_3, edge_attr_4, edge_attr_64, edge_attr_8, node_vec1, L0_gnn_W_skip0, L0_gnn_W_skip1,
           L0_gnn_W_nl0, L0_gnn_W_nl1, L0_gnn_W_fc1, L0_gnn_W_fc2, L0_gnn_W_out_s, L0_gnn_W_out_v, L1_gnn_W_sc_s,
           L1_gnn_W_sc_v, L1_gnn_W1_s, L1_gnn_W1_v, L1_gnn_W2_s, L1_gnn_W2_v, L1_gnn_W3, L1_gnn_fcW1, L1_gnn_fcW2):
    import numpy as np
    import concourse.bacc as bacc
    from concourse import mybir as mb
    from concourse.bass_utils import run_bass_kernel_spmd

    f32 = np.float32

    def spread(w, width=3):
        w = np.asarray(w)
        m, k = w.shape
        a = np.zeros((m, 3, k, width), f32)
        for c in range(width):
            a[:, c % 3, :, c] = w
        return a.reshape(3 * m, width * k)

    def padded(a, n, value=0):
        a = np.asarray(a)
        b = np.full((n,) + a.shape[1:], value, a.dtype)
        b[:a.shape[0]] = a
        return b

    def blocks(width, *parts):
        a = np.zeros((128, width), f32)
        for row, col, part in parts:
            a[row:row + part.shape[0], col:col + part.shape[1]] = part
        return a

    def by_tile(a):
        return np.ascontiguousarray(a.reshape(2 * PAIRS, TILE, -1).transpose(1, 0, 2).reshape(TILE, -1))

    src_p, dst_p = (padded(a, EDGES, N_NODES).astype(np.int32) for a in (src, dst))
    out_v = np.asarray(L0_gnn_W_out_v)
    out_s, fc2_0, nl0 = np.asarray(L0_gnn_W_out_s), np.asarray(L0_gnn_W_fc2), np.asarray(L0_gnn_W_nl0)
    fc2_1, w1_s = np.asarray(L1_gnn_fcW2), np.asarray(L1_gnn_W1_s)
    w2_s, w2_v, w3 = np.asarray(L1_gnn_W2_s), np.asarray(L1_gnn_W2_v), np.asarray(L1_gnn_W3)
    arrays = {
        "x_rows": np.concatenate([padded(x, NODES), padded(node_vec1, NODES)], axis=1),
        "src_cols": by_tile(src_p), "dst_cols": by_tile(dst_p),
        "src_rows": src_p.reshape(PAIRS, 2 * TILE), "dst_rows": dst_p.reshape(PAIRS, 2 * TILE),
        "edge_vec": by_tile(padded(edge_attr_3, EDGES, 1)),
        "edge_y": by_tile(padded(edge_attr_4, EDGES)),
        "hidden_in_0": padded(edge_attr_64, EDGES).T, "hidden_in_1": padded(edge_attr_8, EDGES).T,
        "fc1_0": L0_gnn_W_fc1, "fc2_in_s_0": blocks(224 + S, (0, 0, fc2_0), (64, 224, nl0)), "in_v_0": spread(L0_gnn_W_nl1, 5),
        "out_sa_0": blocks(128, (0, V, out_s[0:64]), (64, 0, out_v[0:64])),
        "out_dc_0": blocks(OUT0, (0, 0, out_s[64:96]), (32, 96, spread(out_v[96:128]))), "out_b_0": spread(out_v[64:96]),
        "fc1_1": L1_gnn_fcW1, "fc2_in_s_1": blocks(192 + S, (0, 0, fc2_1), (64, 192, w1_s)), "in_v_1": spread(L1_gnn_W1_v),
        "out_sa_1": blocks(V + OUT1, (0, V, w3[0:64]), (0, V + 1, w2_s[0:64]), (64, 0, w2_v[0:64])),
        "out_db_1": blocks(OUT1, (0, 0, w3[64:96]), (0, 1, w2_s[64:96]), (32, 1 + S, spread(w2_v[64:96]))),
        "skip_s_0": L0_gnn_W_skip0, "skip_v_0": spread(L0_gnn_W_skip1),
        "skip_s_1": padded(np.asarray(L1_gnn_W_sc_s).T, D).T, "skip_v_1": spread(L1_gnn_W_sc_v),
    }
    nc = bacc.Bacc("TRN2", target_bir_lowering=False, num_devices=1)
    feeds, t_in = {}, {}
    for name, a in arrays.items():
        a = np.ascontiguousarray(np.asarray(a))
        feeds["in_" + name] = a
        t_in[name] = nc.dram_tensor("in_" + name, list(a.shape), mb.dt.from_np(a.dtype), kind="ExternalInput").ap()
    out = nc.dram_tensor("out_rows", [NODES, D], mb.dt.float32, kind="ExternalOutput").ap()
    build_gnn(nc, t_in, out)
    r = run_bass_kernel_spmd(nc, [feeds], core_ids=[0])
    return r.results[0]["out_rows"][:N_NODES]
```
